# Optimizing a Trainium2 kernel written in Bass

```python
import numpy as np
import jax
import jax.numpy as jnp

def _softmax(x, axis=-1):
    return jax.nn.softmax(x, axis=axis)

def _gelu(x):
    return jax.nn.gelu(x, approximate=True)

def _silu(x):
    return jax.nn.silu(x)

def _sigmoid(x):
    return jax.nn.sigmoid(x)

def _layernorm(x, axis=-1, eps=1e-05):
    m = jnp.mean(x, axis=axis, keepdims=True)
    v = jnp.var(x, axis=axis, keepdims=True)
    return (x - m) / jnp.sqrt(v + eps)

def _scatter_add(tgt, idx, src, axis=0):
    return tgt.at[idx].add(src)

def _segment_sum(src, seg, n):
    return jax.ops.segment_sum(src, seg, n)
kernel_name = 'mk_adaln_attn_ffn_d1_seqx_r8_3f3c92'

def setup_inputs(seed: int=0):
    np.random.seed(seed)
    _w = jnp.asarray

    def _rec_inputs():
        import jax
        import jax.numpy as jnp
        _rk = jax.random.key(seed)
        x = -0.000125 + 0.9999 * jax.random.normal(jax.random.fold_in(_rk, 1), (8, 128, 512), jnp.float32)
        _lenS = 128 - jax.random.randint(jax.random.fold_in(_rk, 7), (8,), 0, max(1, 128 // 4) + 1, jnp.int32)
        _lenS2 = 128 - jax.random.randint(jax.random.fold_in(_rk, 8), (8,), 0, max(1, 128 // 4) + 1, jnp.int32)
        itok_B_3_7 = jax.random.randint(jax.random.fold_in(_rk, 11), (8,), 3, 8, jnp.int32)
        itok_B_0_2 = jax.random.randint(jax.random.fold_in(_rk, 12), (8,), 0, 3, jnp.int32)
        return (x, itok_B_3_7, itok_B_0_2)
    x, itok_B_3_7, itok_B_0_2 = _rec_inputs()

    def _L0_cond_setup():
        import jax, jax.numpy as jnp
        import numpy as np
        MAX_LORAS, OUT, IN = (8, 512, 512)
        B, S = (4, 256)
        key = jax.random.key(seed)
        k1, k2, k3 = jax.random.split(key, 3)
        x = jax.random.normal(k1, (B, S, IN), dtype=jnp.float32)
        weight = jax.random.normal(k2, (MAX_LORAS, OUT, IN), dtype=jnp.float32) * 0.02
        adapter_ids = jax.random.randint(k3, (B,), 0, MAX_LORAS, dtype=jnp.int32)
        return {'x': x, 'weight': weight, 'adapter_ids': adapter_ids}
    _L0_cond_all = _L0_cond_setup()
    _L0_cond_in = {k: v for k, v in _L0_cond_all.items() if k in ('weight',)}
    del _L0_cond_all

    def _L0_attn_setup():
        import jax, jax.numpy as jnp
        import numpy as np
        D_IN = 512
        D_OUT = 512
        HEADS = 32
        KV_GROUPS = 8
        HEAD_DIM = D_OUT // HEADS
        GROUP_SIZE = HEADS // KV_GROUPS
        CONTEXT_LEN = 512
        ROPE_BASE = 10000.0
        BATCH, TOKENS = (1, 256)

        def _rope_tables(context_length, head_dim, theta_base):
            inv_freq = 1.0 / theta_base ** (np.arange(0, head_dim, 2)[:head_dim // 2].astype(np.float32) / head_dim)
            pos = np.arange(context_length, dtype=np.float32)
            angles = pos[:, None] * inv_freq[None, :]
            angles = np.concatenate([angles, angles], axis=1)
            return (jnp.asarray(np.cos(angles), jnp.float32), jnp.asarray(np.sin(angles), jnp.float32))

        def _apply_rope(x, cos, sin):
            hd = x.shape[-1]
            x1, x2 = (x[..., :hd // 2], x[..., hd // 2:])
            rotated = jnp.concatenate([-x2, x1], axis=-1)
            return x * cos + rotated * sin
        key = jax.random.key(seed)
        kx, kq, kk, kv, ko = jax.random.split(key, 5)
        s = 0.02
        x = jax.random.normal(kx, (BATCH, TOKENS, D_IN), jnp.float32)
        Wq = jax.random.normal(kq, (D_IN, D_OUT), jnp.float32) * s
        Wk = jax.random.normal(kk, (D_IN, KV_GROUPS * HEAD_DIM), jnp.float32) * s
        Wv = jax.random.normal(kv, (D_IN, KV_GROUPS * HEAD_DIM), jnp.float32) * s
        Wo = jax.random.normal(ko, (D_OUT, D_OUT), jnp.float32) * s
        cos, sin = _rope_tables(CONTEXT_LEN, HEAD_DIM, ROPE_BASE)
        return {'x': x, 'Wq': Wq, 'Wk': Wk, 'Wv': Wv, 'Wo': Wo, 'cos': cos, 'sin': sin}
    _L0_attn_all = _L0_attn_setup()
    _L0_attn_in = {k: v for k, v in _L0_attn_all.items() if k in ('Wq', 'Wk', 'Wv', 'Wo', 'cos', 'sin')}
    del _L0_attn_all

    def _L0_cond2_setup():
        import jax, jax.numpy as jnp
        import numpy as np
        B, S, D_IN, D_OUT = (4, 256, 512, 512)
        R, NUM_LABELERS = (32, 5)
        LORA_SCALING = 16 / 32
        key = jax.random.key(seed)
        k1, k2, k3, k4, k5 = jax.random.split(key, 5)
        x = jax.random.normal(k1, (B, S, D_IN), dtype=jnp.float32)
        labeler_index = jax.random.randint(k2, (B,), 0, NUM_LABELERS, dtype=jnp.int64)
        W = jax.random.normal(k3, (D_OUT, D_IN), dtype=jnp.float32) * 0.02
        lora_A = jax.random.normal(k4, (NUM_LABELERS, D_IN, R), dtype=jnp.float32) * 0.02
        lora_B_w = jax.random.normal(k5, (D_OUT, R), dtype=jnp.float32) * 0.02
        return {'x': x, 'labeler_index': labeler_index, 'W': W, 'lora_A': lora_A, 'lora_B_w': lora_B_w}
    _L0_cond2_all = _L0_cond2_setup()
    _L0_cond2_in = {k: v for k, v in _L0_cond2_all.items() if k in ('W', 'lora_A', 'lora_B_w')}
    del _L0_cond2_all

    def _L0_ffn_setup():
        import jax, jax.numpy as jnp
        import numpy as np
        NUM_EXPERTS = 8
        TOP_K = 2
        RANK = 16
        LORA_ALPHA = 32
        SCALING = LORA_ALPHA / RANK
        key = jax.random.key(seed)
        ks = jax.random.split(key, 6)
        B, S, D_IN, D_OUT = (4, 256, 512, 512)
        x = jax.random.normal(ks[0], (B, S, D_IN), dtype=jnp.float32)
        W_base = jax.random.normal(ks[1], (D_OUT, D_IN), dtype=jnp.float32) * 0.02
        b_base = jax.random.normal(ks[2], (D_OUT,), dtype=jnp.float32) * 0.02
        W_router = jax.random.normal(ks[3], (NUM_EXPERTS, D_IN), dtype=jnp.float32) * 0.02
        A = jax.random.normal(ks[4], (NUM_EXPERTS, RANK, D_IN), dtype=jnp.float32) * 0.02
        Bm = jax.random.normal(ks[5], (D_OUT, RANK), dtype=jnp.float32) * 0.02
        Bm = jnp.broadcast_to(Bm, (NUM_EXPERTS, D_OUT, RANK)) * jnp.arange(1, NUM_EXPERTS + 1, dtype=jnp.float32)[:, None, None] * 0.2
        return {'x': x, 'W_base': W_base, 'b_base': b_base, 'W_router': W_router, 'A': A, 'B': Bm}
    _L0_ffn_all = _L0_ffn_setup()
    _L0_ffn_in = {k: v for k, v in _L0_ffn_all.items() if k in ('W_base', 'b_base', 'W_router', 'A', 'B')}
    del _L0_ffn_all
    return {'x': x, 'itok_B_3_7': itok_B_3_7, 'itok_B_0_2': itok_B_0_2, 'L0_cond_weight': _L0_cond_in['weight'], 'L0_attn_Wq': _L0_attn_in['Wq'], 'L0_attn_Wk': _L0_attn_in['Wk'], 'L0_attn_Wv': _L0_attn_in['Wv'], 'L0_attn_Wo': _L0_attn_in['Wo'], 'L0_attn_cos': _L0_attn_in['cos'], 'L0_attn_sin': _L0_attn_in['sin'], 'L0_cond2_W': _L0_cond2_in['W'], 'L0_cond2_lora_A': _L0_cond2_in['lora_A'], 'L0_cond2_lora_B_w': _L0_cond2_in['lora_B_w'], 'L0_ffn_W_base': _L0_ffn_in['W_base'], 'L0_ffn_b_base': _L0_ffn_in['b_base'], 'L0_ffn_W_router': _L0_ffn_in['W_router'], 'L0_ffn_A': _L0_ffn_in['A'], 'L0_ffn_B': _L0_ffn_in['B']}

def reference(x, itok_B_3_7, itok_B_0_2, L0_cond_weight, L0_attn_Wq, L0_attn_Wk, L0_attn_Wv, L0_attn_Wo, L0_attn_cos, L0_attn_sin, L0_cond2_W, L0_cond2_lora_A, L0_cond2_lora_B_w, L0_ffn_W_base, L0_ffn_b_base, L0_ffn_W_router, L0_ffn_A, L0_ffn_B):
    import jax
    import jax.numpy as jnp

    def _L0_cond_ref(x, weight, adapter_ids):
        import jax, jax.numpy as jnp
        import numpy as np
        MAX_LORAS, OUT, IN = (8, 512, 512)
        B, S = (4, 256)
        w = weight[adapter_ids]
        return jnp.einsum('bsi,boi->bso', x, w)

    def _L0_attn_ref(x, Wq, Wk, Wv, Wo, cos, sin):
        import jax, jax.numpy as jnp
        import numpy as np
        D_IN = 512
        D_OUT = 512
        HEADS = 32
        KV_GROUPS = 8
        HEAD_DIM = D_OUT // HEADS
        GROUP_SIZE = HEADS // KV_GROUPS
        CONTEXT_LEN = 512
        ROPE_BASE = 10000.0
        BATCH, TOKENS = (1, 256)

        def _rope_tables(context_length, head_dim, theta_base):
            inv_freq = 1.0 / theta_base ** (np.arange(0, head_dim, 2)[:head_dim // 2].astype(np.float32) / head_dim)
            pos = np.arange(context_length, dtype=np.float32)
            angles = pos[:, None] * inv_freq[None, :]
            angles = np.concatenate([angles, angles], axis=1)
            return (jnp.asarray(np.cos(angles), jnp.float32), jnp.asarray(np.sin(angles), jnp.float32))

        def _apply_rope(x, cos, sin):
            hd = x.shape[-1]
            x1, x2 = (x[..., :hd // 2], x[..., hd // 2:])
            rotated = jnp.concatenate([-x2, x1], axis=-1)
            return x * cos + rotated * sin
        B, T, _ = x.shape
        q = (x @ Wq).reshape(B, T, HEADS, HEAD_DIM).transpose(0, 2, 1, 3)
        k = (x @ Wk).reshape(B, T, KV_GROUPS, HEAD_DIM).transpose(0, 2, 1, 3)
        v = (x @ Wv).reshape(B, T, KV_GROUPS, HEAD_DIM).transpose(0, 2, 1, 3)
        cos_t, sin_t = (cos[:T], sin[:T])
        q = _apply_rope(q, cos_t, sin_t)
        k = _apply_rope(k, cos_t, sin_t)
        qg = q.reshape(B, KV_GROUPS, GROUP_SIZE, T, HEAD_DIM)
        scores = jnp.einsum('bgptd,bgsd->bgpts', qg, k)
        causal = jnp.triu(jnp.ones((T, T), bool), k=1)
        scores = jnp.where(causal, -jnp.inf, scores)
        weights = jax.nn.softmax(scores / jnp.sqrt(jnp.float32(HEAD_DIM)), axis=-1)
        ctx = jnp.einsum('bgpts,bgsd->bgptd', weights, v)
        ctx = ctx.reshape(B, HEADS, T, HEAD_DIM).transpose(0, 2, 1, 3).reshape(B, T, D_OUT)
        return ctx @ Wo

    def _L0_cond2_ref(x, labeler_index, W, lora_A, lora_B_w):
        import jax, jax.numpy as jnp
        import numpy as np
        B, S, D_IN, D_OUT = (4, 256, 512, 512)
        R, NUM_LABELERS = (32, 5)
        LORA_SCALING = 16 / 32
        base = jnp.einsum('bsi,oi->bso', x, W)
        labelers_A = lora_A[labeler_index]
        low = jnp.einsum('bsi,bir->bsr', x, labelers_A)
        delta = jnp.einsum('bsr,or->bso', low, lora_B_w) * LORA_SCALING
        return base + delta

    def _L0_ffn_ref(x, W_base, b_base, W_router, A, B):
        import jax, jax.numpy as jnp
        import numpy as np
        NUM_EXPERTS = 8
        TOP_K = 2
        RANK = 16
        LORA_ALPHA = 32
        SCALING = LORA_ALPHA / RANK
        bs, seq, d_in = x.shape
        T = bs * seq
        xf = x.reshape(T, d_in)
        base = xf @ W_base.T + b_base
        logits = xf @ W_router.T
        rw, sel = jax.lax.top_k(logits, TOP_K)
        rw = jax.nn.softmax(rw, axis=-1)
        onehot = jax.nn.one_hot(sel, NUM_EXPERTS, dtype=rw.dtype)
        w = jnp.einsum('tk,tke->te', rw, onehot)
        h = jnp.einsum('td,erd->ter', xf, A)
        lora = jnp.einsum('ter,te,eor->to', h, w, B) * SCALING
        return (base + lora).reshape(bs, seq, -1)
    x = x + _L0_attn_ref(_L0_cond_ref(x, L0_cond_weight, itok_B_3_7), L0_attn_Wq, L0_attn_Wk, L0_attn_Wv, L0_attn_Wo, L0_attn_cos, L0_attn_sin)
    x = x + _L0_ffn_ref(_L0_cond2_ref(x, itok_B_0_2, L0_cond2_W, L0_cond2_lora_A, L0_cond2_lora_B_w), L0_ffn_W_base, L0_ffn_b_base, L0_ffn_W_router, L0_ffn_A, L0_ffn_B)
    return x

_drawn_inputs = setup_inputs


def setup_inputs(seed=0):
    import zlib

    import numpy as np

    out = dict(_drawn_inputs(seed))
    spreads = {}
    factors = {'L0_cond_weight': 2.94,
     'L0_attn_Wq': 8.0,
     'L0_attn_Wk': 8.0,
     'L0_attn_Wv': 2.905,
     'L0_attn_Wo': 2.96,
     'L0_attn_cos': 8.0,
     'L0_attn_sin': 8.0,
     'L0_cond2_lora_A': 4.674,
     'L0_cond2_lora_B_w': 4.578,
     'L0_ffn_b_base': 2.905,
     'L0_ffn_W_router': 2.757}
    for name, (base, spread) in spreads.items():
        noise = np.random.default_rng([zlib.crc32(name.encode()), seed]).standard_normal(out[name].shape)
        drawn = base * np.exp(spread * noise) if base else spread * noise
        out[name] = jnp.asarray(drawn.astype(out[name].dtype))
    for name, factor in factors.items():
        out[name] = (out[name] * factor).astype(out[name].dtype)
    return out
```

```python
from contextlib import ExitStack

import concourse.bass as bass
from concourse import mybir

ALU = mybir.AluOpType
ACT = mybir.ActivationFunctionType
AX_X = mybir.AxisListType.X
F32 = mybir.dt.float32
F32R = mybir.dt.float32r
BF16 = mybir.dt.bfloat16
U32 = mybir.dt.uint32
I32 = mybir.dt.int32

P = 128
MASKED = -3.0e38


def build_program(nc, x, x_t, cond_ids, lora_ids, cond_w_t, w_q, w_kv, w_o, cos, sin, w2_t, lora_a, lora_b_t,
                  base_t, base_bias, router_t, experts_a_t, experts_b, out):
    BATCH, T, D = x.shape
    assert T == P
    KT = D // P
    HD = cos.shape[1]
    KV = w_kv.shape[1] // 2
    GROUPS = KV // HD
    PER = D // KV
    HEADS = GROUPS * PER
    PAIRS = GROUPS // 2
    assert KV == P and 2 * HD == 32
    CHUNKS = 2 * PER
    EXPERTS = router_t.shape[1]
    RANK = experts_a_t.shape[1] // EXPERTS
    LR = lora_a.shape[2]
    GATES = EXPERTS + EXPERTS * RANK
    NCOND, NLORA = cond_w_t.shape[0], lora_a.shape[0]
    QK = D + KV
    QKV = D + 2 * KV
    FFN = GATES + D
    SCORE_SCALE = float(HD) ** -0.5
    LORA_SCALE = 16 / 32
    MOE_SCALE = 32 / 16

    with ExitStack() as ctx:
        def sb(name, shape, dt=F32):
            return ctx.enter_context(nc.sbuf_tensor(name, shape, dt))

        def sem(name):
            return ctx.enter_context(nc.semaphore(name))

        class Pair:

            def __init__(self, name, shape):
                self.hi, self.lo = sb(name + "_hi", shape, F32R), sb(name + "_lo", shape, F32R)

        bank = [ctx.enter_context(nc.psum_tensor(f"bank{i}", [P, 512], F32)) for i in range(8)]
        scores_ps = bank[0:2]
        probs_t_ps = bank[2:4]
        ctx_ps = bank[4]
        x_ps = bank[5]
        y_ps = bank[6]
        z_ps = bank[7]

        qkv_w = Pair("qkv_w", [P, KT, QKV])
        o_w = Pair("o_w", [P, KT, D])
        w2 = Pair("w2", [P, KT, D])
        ffn_w = Pair("ffn_w", [P, KT, FFN])
        lora_b = Pair("lora_b", [P, D])
        moe_b = Pair("moe_b", [P, D])
        stage_a = sb("stage_a", [P, KT * QKV])
        stage_b = sb("stage_b", [P, KT * D])
        spare = sb("spare", [P, 2, D])
        stage_c = spare
        cond_raw = sb("cond_raw", [P, KT, D])
        cond_w = Pair("cond_w", [P, KT, D])
        a_raw = sb("a_raw", [P, KT, LR])
        lora_aw = Pair("lora_aw", [P, KT, P])
        bias_row = sb("bias_row", [P, D])
        ids = sb("ids", [1, 2 * BATCH], I32)

        ident = sb("ident", [P, P])
        ident_bf = sb("ident_bf", [P, P], BF16)
        causal = sb("causal", [P, 4, P], BF16)
        own_group = sb("own_group", [P, GROUPS])
        rope_cos = sb("rope_cos", [P, HD])
        rope_sin = sb("rope_sin", [P, HD])
        expert_no = sb("expert_no", [P, EXPERTS])

        xt_raw = sb("xt_raw", [P, KT, P])
        xt = Pair("xt", [P, KT, P])
        x_nat = sb("x_nat", [P, D])
        turn = sb("turn", [P, D])
        c_t = Pair("c_t", [P, KT, P])
        rope_a = sb("rope_a", [P, QK])
        rope_b = sb("rope_b", [P, QK])
        qk = sb("qk", [P, QK])
        q_t = Pair("q_t", [P, PER, P])
        k_t = Pair("k_t", [P, P])
        k_diag = Pair("k_diag", [P, GROUPS, P])
        v_pad = [sb(f"v_pad{e}", [P, PAIRS, 2, HD]) for e in range(2)]
        neg_max = sb("neg_max", [P, HEADS])
        sums = sb("sums", [P, HEADS])
        inv_sum = sb("inv_sum", [P, HEADS])
        probs = [sb(f"probs{i}", [P, PAIRS, P]) for i in range(2)]
        probs_t = [sb(f"probs_t{i}", [P, PAIRS, P]) for i in range(2)]
        inv_wide, ctx_n = spare[:, 0, :], spare[:, 1, :]
        inv_t = rope_a[:, 0:D]
        ctx_t = Pair("ctx_t", [P, PER, P])
        x1 = sb("x1", [P, D])
        x1_bias = sb("x1_bias", [P, D])
        x1_t = Pair("x1_t", [P, KT, P])
        low_t = Pair("low_t", [P, P])
        c2_t = Pair("c2_t", [P, KT, P])
        logits = sb("logits", [P, EXPERTS])
        top = sb("top", [P, 8])
        top_at = sb("top_at", [P, 8], U32)
        top_no = sb("top_no", [P, 2])
        neg_top = sb("neg_top", [P, 1])
        top_less = sb("top_less", [P, 2])
        top_exp = sb("top_exp", [P, 2])
        top_sum = sb("top_sum", [P, 1])
        top_inv = sb("top_inv", [P, 1])
        top_w = sb("top_w", [P, 2])
        pick = sb("pick", [P, 2, EXPERTS])
        gate = sb("gate", [P, EXPERTS])
        hidden = sb("hidden", [P, EXPERTS * RANK])
        hidden_t = Pair("hidden_t", [P, P])
        out_sb = sb("out_sb", [P, D])

        ids_in, tables_in, bias_in = sem("ids_in"), sem("tables_in"), sem("bias_in")
        cond_in, xt_in, x_in, a_in = sem("cond_in"), sem("xt_in"), sem("x_in"), sem("a_in")
        qkv_in, o_in, w2_in, ffn_in, b_in = sem("qkv_in"), sem("o_in"), sem("w2_in"), sem("ffn_in"), sem("b_in")
        out_free = sem("out_free")
        zeroed, tables_made, sin_signed = sem("zeroed"), sem("tables_made"), sem("sin_signed")
        qkv_hi, o_hi, w2_hi, ffn_hi, b_hi = sem("qkv_hi"), sem("o_hi"), sem("w2_hi"), sem("ffn_hi"), sem("b_hi")
        qkv_lo, o_lo, w2_lo, ffn_lo, b_lo = sem("qkv_lo"), sem("o_lo"), sem("w2_lo"), sem("ffn_lo"), sem("b_lo")
        cond_hi, cond_lo, xt_hi, xt_lo = sem("cond_hi"), sem("cond_lo"), sem("xt_hi"), sem("xt_lo")
        a_hi, a_lo = sem("a_hi"), sem("a_lo")
        c_done, c_copied, ct_done, ct_hi, ct_lo = (sem("c_done"), sem("c_copied"), sem("ct_done"), sem("ct_hi"),
                                                   sem("ct_lo"))
        qkv_done, rope_mul, v_ready, qk_ready = sem("qkv_done"), sem("rope_mul"), sem("v_ready"), sem("qk_ready")
        kt_done, qt_done, kt_hi, kt_lo = sem("kt_done"), sem("qt_done"), sem("kt_hi"), sem("kt_lo")
        kd_hi, kd_lo, qt_hi, qt_lo = sem("kd_hi"), sem("kd_lo"), sem("qt_hi"), sem("qt_lo")
        scored, maxed, exped, pt_done = sem("scored"), sem("maxed"), sem("exped"), sem("pt_done")
        pt_even, pt_odd, ctx_done = sem("pt_even"), sem("pt_odd"), sem("ctx_done")
        inverted, inv_ready, inv_t_done, inv_t_ready = (sem("inverted"), sem("inv_ready"), sem("inv_t_done"),
                                                        sem("inv_t_ready"))
        ctx_normed, ctx_hi, ctx_lo = sem("ctx_normed"), sem("ctx_hi"), sem("ctx_lo")
        attn_done, x1_ready, x1b_ready = sem("attn_done"), sem("x1_ready"), sem("x1b_ready")
        x1t_done, x1t_hi, x1t_lo = sem("x1t_done"), sem("x1t_hi"), sem("x1t_lo")
        low_done, low_hi, low_lo = sem("low_done"), sem("low_hi"), sem("low_lo")
        c2_done, c2_copied, c2t_done, c2t_hi, c2t_lo = (sem("c2_done"), sem("c2_copied"), sem("c2t_done"),
                                                        sem("c2t_hi"), sem("c2t_lo"))
        gates_done, gating, top_exped, hidden_ready = (sem("gates_done"), sem("gating"), sem("top_exped"),
                                                       sem("hidden_ready"))
        ht_done, ht_hi, ht_lo, ffn_done, out_ready = (sem("ht_done"), sem("ht_hi"), sem("ht_lo"), sem("ffn_done"),
                                                      sem("out_ready"))

        f32 = lambda ap: ap.bitcast(F32)
        flat = lambda t: t[:, :, :].rearrange("p a b -> p (a b)")

        def iterations(eng, iteration):
            iteration(-1, front=True, attend=False, back=False)
            iteration(0, front=True, attend=True, back=False)
            with eng.Fori(1, BATCH - 1) as t:
                iteration(t, front=True, attend=True, back=True)
            iteration(BATCH - 1, front=False, attend=True, back=True)
            iteration(BATCH, front=False, attend=False, back=True)

        block = ctx.enter_context(nc.Block())

        @block.sync
        def _(sp):
            def load_cond(f, n):
                sp.dma_start(cond_raw[:, :, :], cond_w_t[bass.ds(n, 1), :, :].rearrange("a (k p) o -> p (a k) o", p=P)
                             ).then_inc(cond_in, 16)
                sp.dma_start(xt_raw[:, :, :], x_t[bass.ds(f, 1), :, :].rearrange("a (k p) s -> p (a k) s", p=P)
                             ).then_inc(xt_in, 16)

            def iteration(t, front, attend, back):
                f, r = t + 1, t - 1
                if front:
                    n = sp.value_load(ids[0:1, bass.ds(f, 1)], min_val=0, max_val=NCOND - 1)
                    if attend:
                        sp.wait_ge(cond_lo, KT * f)
                        sp.wait_ge(xt_lo, f)
                        sp.wait_ge(ids_in, 32)
                    load_cond(f, n)
                if not attend and front:
                    stage_qkv = stage_a[:, :].rearrange("p (k n) -> p k n", k=KT)
                    sp.dma_start(stage_qkv[:, :, 0:D], w_q.rearrange("(k p) n -> p k n", p=P)).then_inc(qkv_in, 16)
                    sp.dma_start(stage_qkv[:, :, D:QKV], w_kv.rearrange("(k p) n -> p k n", p=P)).then_inc(qkv_in, 16)
                    sp.dma_start(rope_cos[:, :], cos[0:P, :]).then_inc(tables_in, 16)
                    sp.dma_start(rope_sin[:, :], sin[0:P, :]).then_inc(tables_in, 16)
                if attend and not back:
                    stage_3 = stage_b[:, :].rearrange("p (k n) -> p k n", k=KT)
                    sp.dma_start(stage_3, w_o.rearrange("(k p) n -> p k n", p=P)).then_inc(o_in, 16)
                    sp.dma_start(bias_row[:, :], base_bias.partition_broadcast(P)).then_inc(bias_in, 16)
                    sp.dma_start(stage_c[0:LR, 0, :], lora_b_t).then_inc(b_in, 16)
                    sp.dma_start(stage_c[:, 1, :], experts_b).then_inc(b_in, 16)
                    sp.wait_ge(qkv_lo, 1)
                    stage_ffn = stage_a[:, 0:KT * FFN].rearrange("p (k n) -> p k n", k=KT)
                    for src, at in ((router_t, 0), (experts_a_t, EXPERTS), (base_t, GATES)):
                        sp.dma_start(stage_ffn[:, :, at:at + src.shape[1]], src.rearrange("(k p) n -> p k n", p=P)
                                     ).then_inc(ffn_in, 16)
                    sp.wait_ge(o_lo, 1)
                    sp.dma_start(stage_3, w2_t.rearrange("(k p) n -> p k n", p=P)).then_inc(w2_in, 16)
                if attend:
                    n = sp.value_load(ids[0:1, bass.ds(t + BATCH, 1)], min_val=0, max_val=NLORA - 1)
                    if back:
                        sp.wait_ge(x1_ready, t)
                        sp.wait_ge(a_lo, t)
                        sp.wait_ge(ids_in, 32)
                    sp.dma_start(x_nat[:, :], x[bass.ds(t, 1), :, :].rearrange("a s d -> s (a d)")).then_inc(x_in, 16)
                    sp.dma_start(a_raw[:, :, :], lora_a[bass.ds(n, 1), :, :].rearrange("a (k p) r -> p (a k) r", p=P)
                                 ).then_inc(a_in, 16)
                if back:
                    sp.wait_ge(out_ready, r + 1)
                    sp.wait_ge(ids_in, 32)
                    sp.dma_start(out[bass.ds(r, 1), :, :].rearrange("a s d -> s (a d)"), out_sb[:, :]
                                 ).then_inc(out_free, 16)

            sp.dma_start(ids[0:1, 0:BATCH], cond_ids.rearrange("(a n) -> a n", a=1)).then_inc(ids_in, 16)
            sp.dma_start(ids[0:1, BATCH:2 * BATCH], lora_ids.rearrange("(a n) -> a n", a=1)).then_inc(ids_in, 16)
            sp.wait_ge(ids_in, 32)
            iterations(sp, iteration)
            sp.wait_ge(out_free, 16 * (BATCH + 1))

        @block.gpsimd
        def _(pool):
            def subtract(pair, raw, hi_at=slice(None)):
                return pool.tensor_tensor(pair.lo, raw, f32(pair.hi), ALU.subtract)

            def tables():
                pool.memset(ident[:, :], 0.0).then_inc(zeroed, 1)
                pool.memset(ident_bf[:, :], 0.0).then_inc(zeroed, 1)
                pool.memset(causal[:, :, :], 0.0).then_inc(zeroed, 1)
                pool.memset(own_group[:, :], 1.0).then_inc(zeroed, 1)
                for e in range(2):
                    pool.memset(v_pad[e][:, :, :, :], 0.0).then_inc(zeroed, 1)
                for half in (lora_b.hi, lora_b.lo):
                    pool.memset(half[:, :].bitcast(F32), 0.0).then_inc(zeroed, 1)
                for half in (lora_aw.hi, lora_aw.lo):
                    pool.memset(half[:, :, :].bitcast(F32), 0.0).then_inc(zeroed, 1)
                pool.iota(expert_no[:, :], [[1, EXPERTS]], base=0, channel_multiplier=0,
                          allow_small_or_imprecise_dtypes=True).then_inc(zeroed, 1)
                pool.memset(out_sb[:, :], 0.0).then_inc(out_free, 16)
                pool.wait_ge(zeroed, 4)
                for tile in (ident, ident_bf):
                    pool.affine_select(out=tile[:, :], in_=tile[:, :], compare_op=ALU.not_equal, fill=1.0, base=0,
                                       pattern=[[-1, P]], channel_multiplier=1).then_inc(tables_made, 1)
                pool.affine_select(out=causal[:, :, :], in_=causal[:, :, :], compare_op=ALU.is_ge, fill=MASKED,
                                   base=0, pattern=[[0, 4], [-1, P]], channel_multiplier=1).then_inc(tables_made, 1)
                grp = own_group[:, :].rearrange("p (e j) -> p e j", e=2)
                pool.affine_select(out=grp, in_=grp, compare_op=ALU.is_ge, fill=0.0, base=0,
                                   pattern=[[-HD, 2], [-2 * HD, PAIRS]], channel_multiplier=1
                                   ).then_inc(tables_made, 1)
                pool.wait_ge(tables_made, 4)
                pool.affine_select(out=grp, in_=grp, compare_op=ALU.is_ge, fill=0.0, base=HD - 1,
                                   pattern=[[HD, 2], [2 * HD, PAIRS]], channel_multiplier=-1
                                   ).then_inc(tables_made, 1)

            def split_cond(f, guard):
                pool.wait_ge(xt_hi, f + 1)
                pool.tensor_tensor(xt.lo[:, :, :], xt_raw[:, :, :], f32(xt.hi[:, :, :]), ALU.subtract
                                   ).then_inc(xt_lo, 1)
                for k in range(KT):
                    pool.wait_ge(cond_hi, KT * f + k + 1)
                    pool.tensor_tensor(cond_w.lo[:, k, :], cond_raw[:, k, :], f32(cond_w.hi[:, k, :]), ALU.subtract
                                       ).then_inc(cond_lo, 1)

            def iteration(t, front, attend, back):
                f, r = t + 1, t - 1
                if attend:
                    pool.wait_ge(kt_lo, t + 1)
                    pool.tensor_tensor(k_diag.lo[:, :, :],
                                       f32(k_t.lo[:, :]).unsqueeze(1).broadcast_to([P, GROUPS, P]),
                                       own_group[:, :].unsqueeze(2).broadcast_to([P, GROUPS, P]), ALU.mult
                                       ).then_inc(kd_lo, 1)
                if back:
                    pool.wait_ge(a_hi, r + 1)
                    pool.tensor_tensor(lora_aw.lo[:, :, 0:LR], a_raw[:, :, :], f32(lora_aw.hi[:, :, 0:LR]),
                                       ALU.subtract).then_inc(a_lo, 1)
                    pool.wait_ge(bias_in, 16)
                    pool.wait_ge(x1_ready, r + 1)
                    pool.tensor_tensor(x1_bias[:, :], x1[:, :], bias_row[:, :], ALU.add).then_inc(x1b_ready, 1)
                if front:
                    split_cond(f, attend)
                    pool.wait_ge(rope_mul, f + 1)
                    pool.tensor_tensor(qk[:, :], rope_a[:, :], rope_b[:, :], ALU.add).then_inc(qk_ready, 1)

            tables()
            iterations(pool, iteration)

        @block.scalar
        def _(act):
            def copy(out, in_, scale=1.0):
                return nc.scalar.activation(out, in_, ACT.Copy, scale=scale)

            def exp_chunk(t, c):
                act.wait_ge(maxed, CHUNKS * t + c + 1)
                if c >= 2:
                    act.wait_ge(pt_done, CHUNKS * t + c - 1)
                p, e = c // 2, c % 2
                for j in range(PAIRS):
                    h = p * GROUPS + 2 * j + e
                    last = nc.scalar.activation(probs[c % 2][:, j, :], scores_ps[c % 2][:, j * P:(j + 1) * P],
                                                ACT.Exp, bias=neg_max[:, h:h + 1], accum_out=sums[:, h:h + 1])
                last.then_inc(exped, 1)

            def evacuate_odd(t, c):
                act.wait_ge(pt_done, CHUNKS * t + c + 1)
                if c >= 2:
                    act.wait_ge(ctx_done, CHUNKS * t + c - 1)
                copy(probs_t[1][:, :, :], probs_t_ps[1][:, :]).then_inc(pt_odd, 1)

            def iteration(t, front, attend, back):
                f, r = t + 1, t - 1
                if attend:
                    act.wait_ge(kt_done, t + 1)
                    if back:
                        act.wait_ge(kd_lo, t)
                    copy(k_t.hi[:, :], y_ps[:, 0:P]).then_inc(kt_hi, 1)
                if back:
                    act.wait_ge(inv_t_done, r + 1)
                    copy(inv_t, probs_t_ps[0][:, :]).then_inc(inv_t_ready, 1)
                if attend:
                    act.wait_ge(qt_done, t + 1)
                    copy(flat(q_t.hi), x_ps[:, :], SCORE_SCALE).then_inc(qt_hi, 1)
                if back:
                    act.wait_ge(a_in, 16 * (r + 1))
                    copy(lora_aw.hi[:, :, 0:LR], a_raw[:, :, :]).then_inc(a_hi, 1)
                    act.wait_ge(inv_ready, r + 1)

                def slot(c):
                    if attend:
                        exp_chunk(t, c)
                        if c >= 2 and c % 2 == 0:
                            evacuate_odd(t, c - 1)
                    if c == 0 and front:
                        act.wait_ge(xt_in, 16 * (f + 1))
                        if attend:
                            act.wait_ge(c_done, f)
                        copy(flat(xt.hi), flat(xt_raw)).then_inc(xt_hi, 1)
                    if c < KT and front:
                        act.wait_ge(cond_in, 16 * (f + 1))
                        copy(cond_w.hi[:, c, :], cond_raw[:, c, :]).then_inc(cond_hi, 1)
                    if c == 3 and not attend and front:
                        act.wait_ge(qkv_in, 32)
                        copy(flat(qkv_w.hi), stage_a[:, :]).then_inc(qkv_hi, 1)
                    if c == 3 and attend and not back:
                        act.wait_ge(o_in, 16)
                        copy(flat(o_w.hi), stage_b[:, :]).then_inc(o_hi, 1)
                    if c == 4 and attend and not back:
                        act.wait_ge(ffn_in, 48)
                        copy(flat(ffn_w.hi), stage_a[:, 0:KT * FFN]).then_inc(ffn_hi, 1)
                    if c == 6 and attend and not back:
                        act.wait_ge(w2_in, 16)
                        copy(flat(w2.hi), stage_b[:, :]).then_inc(w2_hi, 1)
                        act.wait_ge(b_in, 32)
                        act.wait_ge(zeroed, 11)
                        copy(lora_b.hi[0:LR, :], stage_c[0:LR, 0, :]).then_inc(b_hi, 1)
                        copy(moe_b.hi[:, :], stage_c[:, 1, :]).then_inc(b_hi, 1)
                    if c == 1 and back:
                        act.wait_ge(x1t_done, r + 1)
                        copy(flat(x1_t.hi), x_ps[:, :]).then_inc(x1t_hi, 1)
                    if c == 2 and back:
                        act.wait_ge(low_done, r + 1)
                        copy(low_t.hi[:, :], y_ps[:, 0:P], LORA_SCALE).then_inc(low_hi, 1)
                    if c == 3 and back:
                        act.wait_ge(c2_done, r + 1)
                        copy(turn[:, :], z_ps[:, :]).then_inc(c2_copied, 1)
                    if c == 4 and back:
                        act.wait_ge(c2t_done, r + 1)
                        copy(flat(c2_t.hi), x_ps[:, :]).then_inc(c2t_hi, 1)
                    if c == 6 and front:
                        act.wait_ge(c_done, f + 1)
                        copy(turn[:, :], y_ps[:, :]).then_inc(c_copied, 1)
                    if c == 7 and back:
                        act.wait_ge(gating, 6 * r + 4)
                        nc.scalar.activation(top_exp[:, :], top_less[:, :], ACT.Exp).then_inc(top_exped, 1)
                    if c == 7 and front:
                        act.wait_ge(ct_done, f + 1)
                        copy(flat(c_t.hi), y_ps[:, :]).then_inc(ct_hi, 1)

                for c in range(CHUNKS):
                    slot(c)
                if back:
                    act.wait_ge(ht_done, r + 1)
                    copy(hidden_t.hi[:, :], scores_ps[0][:, 0:P]).then_inc(ht_hi, 1)
                if attend:
                    evacuate_odd(t, CHUNKS - 1)

            iterations(act, iteration)

        @block.vector
        def _(dve):
            def low_of(pair_lo, value, pair_hi):
                return nc.vector.tensor_tensor(pair_lo, value, f32(pair_hi), ALU.subtract)

            def max_chunk(t, c):
                dve.wait_ge(scored, CHUNKS * t + c + 1)
                p, e = c // 2, c % 2
                heads = neg_max[:, p * GROUPS:(p + 1) * GROUPS].rearrange("q (j e) -> q e j", e=2)[:, e, :]
                nc.vector.tensor_reduce(heads, scores_ps[c % 2][:, :].rearrange("q (j s) -> q j s", s=P), AX_X,
                                        ALU.max, negate=True).then_inc(maxed, 1)

            def evacuate_even(t, c):
                dve.wait_ge(pt_done, CHUNKS * t + c + 1)
                if c >= 2:
                    dve.wait_ge(ctx_done, CHUNKS * t + c - 1)
                nc.vector.tensor_copy(flat(probs_t[0]), probs_t_ps[0][:, :]).then_inc(pt_even, 1)

            def rotate(f, again):
                dve.wait_ge(qkv_done, f + 1)
                if again:
                    dve.wait_ge(qk_ready, f)
                half = HD // 2
                for src, a, n in ((x_ps, 0, HEADS), (y_ps, D, GROUPS)):
                    head = lambda tile, at: tile[:, at:at + n * HD].rearrange("s (h d) -> s h d", d=HD)
                    tab = lambda tile, lo, w: tile[:, lo:lo + w].unsqueeze(1).broadcast_to([P, n, w])
                    nc.vector.tensor_tensor(head(rope_a, a), head(src, 0), tab(rope_cos, 0, HD), ALU.mult)
                    for to, frm in ((0, half), (half, 0)):
                        last = nc.vector.tensor_tensor(head(rope_b, a)[:, :, to:to + half],
                                                       head(src, 0)[:, :, frm:frm + half],
                                                       tab(rope_sin, to, half), ALU.mult)
                last.then_inc(rope_mul, 1)
                if again:
                    dve.wait_ge(ctx_done, CHUNKS * f)
                else:
                    dve.wait_ge(zeroed, 11)
                v = y_ps[:, KV:2 * KV].rearrange("s (j e d) -> s j e d", e=2, d=HD)
                for e in range(2):
                    nc.vector.tensor_copy(v_pad[e][:, :, e, :], v[:, :, e, :]).then_inc(v_ready, 1)

            def invert(r):
                dve.wait_ge(exped, CHUNKS * (r + 1))
                nc.vector.reciprocal(inv_sum[:, :], sums[:, :]).then_inc(inverted, 1)
                dve.wait_ge(inverted, r + 1)
                nc.vector.tensor_copy(inv_wide.rearrange("s (h d) -> s h d", d=HD),
                                      inv_sum[:, :].unsqueeze(2).broadcast_to([P, HEADS, HD])).then_inc(inv_ready, 1)

            def spread_k(t):
                dve.wait_ge(kt_done, t + 1)
                dve.wait_ge(kt_hi, t + 1)
                nc.vector.tensor_tensor(k_t.lo[:, :], y_ps[:, 0:P], f32(k_t.hi[:, :]), ALU.subtract
                                        ).then_inc(kt_lo, 1)
                nc.vector.tensor_tensor(k_diag.hi[:, :, :], y_ps[:, 0:P].unsqueeze(1).broadcast_to([P, GROUPS, P]),
                                        own_group[:, :].unsqueeze(2).broadcast_to([P, GROUPS, P]), ALU.mult
                                        ).then_inc(kd_hi, 1)

            def normalise(r):
                dve.wait_ge(inv_t_ready, r + 1)
                dve.wait_ge(ctx_done, CHUNKS * (r + 1))
                nc.vector.tensor_tensor(ctx_n, ctx_ps[:, :], inv_t, ALU.mult).then_inc(ctx_normed, 1)
                dve.wait_ge(ctx_normed, r + 1)
                nc.vector.tensor_copy(flat(ctx_t.hi), ctx_n).then_inc(ctx_hi, 1)
                dve.wait_ge(ctx_hi, r + 1)
                low_of(flat(ctx_t.lo), ctx_n, flat(ctx_t.hi)).then_inc(ctx_lo, 1)

            def choose_experts(r):
                dve.wait_ge(gates_done, r + 1)
                nc.vector.tensor_copy(logits[:, :], x_ps[:, 0:EXPERTS]).then_inc(gating, 1)
                dve.wait_ge(gating, 6 * r + 1)
                nc.vector.tensor_reduce(neg_top[:, :], logits[:, :], AX_X, ALU.max, negate=True).then_inc(gating, 1)
                nc.vector.max(top[:, :], logits[:, :]).then_inc(gating, 1)
                dve.wait_ge(gating, 6 * r + 3)
                nc.vector.tensor_scalar(top_less[:, :], top[:, 0:2], neg_top[:, 0:1], None, ALU.add
                                        ).then_inc(gating, 1)
                nc.vector.max_index(top_at[:, :], top[:, :], logits[:, :]).then_inc(gating, 1)
                dve.wait_ge(gating, 6 * r + 5)
                nc.vector.tensor_copy(top_no[:, :], top_at[:, 0:2]).then_inc(gating, 1)

            def gate_hidden(r):
                n = 6 * r
                dve.wait_ge(top_exped, r + 1)
                nc.vector.tensor_reduce(top_sum[:, :], top_exp[:, :], AX_X, ALU.add).then_inc(hidden_ready, 1)
                dve.wait_ge(hidden_ready, n + 1)
                nc.vector.reciprocal(top_inv[:, :], top_sum[:, :]).then_inc(hidden_ready, 1)
                dve.wait_ge(hidden_ready, n + 2)
                nc.vector.tensor_scalar(top_w[:, :], top_exp[:, :], top_inv[:, 0:1], MOE_SCALE, ALU.mult, ALU.mult
                                        ).then_inc(hidden_ready, 1)
                dve.wait_ge(hidden_ready, n + 3)
                dve.wait_ge(gating, 6 * r + 6)
                for i in range(2):
                    last = nc.vector.tensor_scalar(pick[:, i, :], expert_no[:, :], top_no[:, i:i + 1],
                                                   top_w[:, i:i + 1], ALU.is_equal, ALU.mult)
                last.then_inc(hidden_ready, 1)
                dve.wait_ge(hidden_ready, n + 4)
                nc.vector.tensor_tensor(gate[:, :], pick[:, 0, :], pick[:, 1, :], ALU.add).then_inc(hidden_ready, 1)
                dve.wait_ge(hidden_ready, n + 5)
                nc.vector.tensor_tensor(hidden[:, :].rearrange("s (e n) -> s e n", n=RANK),
                                        x_ps[:, EXPERTS:GATES].rearrange("s (e n) -> s e n", n=RANK),
                                        gate[:, :].unsqueeze(2).broadcast_to([P, EXPERTS, RANK]), ALU.mult
                                        ).then_inc(hidden_ready, 1)

            def iteration(t, front, attend, back):
                f, r = t + 1, t - 1
                if attend and not back:
                    dve.wait_ge(tables_made, 5)
                if back:
                    invert(r)
                if attend:
                    spread_k(t)
                if back:
                    normalise(r)
                if attend:
                    dve.wait_ge(qt_hi, t + 1)
                    nc.vector.scalar_tensor_tensor(flat(q_t.lo), x_ps[:, :], SCORE_SCALE, f32(flat(q_t.hi)), ALU.mult,
                                                   ALU.subtract).then_inc(qt_lo, 1)
                if back:
                    dve.wait_ge(attn_done, r + 1)
                    dve.wait_ge(x_in, 16 * (r + 1))
                    nc.vector.tensor_tensor(x1[:, :], probs_t_ps[1][:, :], x_nat[:, :], ALU.add).then_inc(x1_ready, 1)

                def slot(c):
                    if attend:
                        max_chunk(t, c)
                        if c >= 1 and c % 2 == 1:
                            evacuate_even(t, c - 1)
                    if c == 3 and not attend and front:
                        dve.wait_ge(tables_in, 32)
                        nc.vector.tensor_scalar(rope_sin[:, 0:HD // 2], rope_sin[:, 0:HD // 2], -1.0, None, ALU.mult
                                                ).then_inc(sin_signed, 1)
                        dve.wait_ge(qkv_hi, 1)
                        low_of(flat(qkv_w.lo), stage_a[:, :], flat(qkv_w.hi)).then_inc(qkv_lo, 1)
                    if c == 4 and attend and not back:
                        dve.wait_ge(o_hi, 1)
                        low_of(flat(o_w.lo), stage_b[:, :], flat(o_w.hi)).then_inc(o_lo, 1)
                    if c == 5 and attend and not back:
                        dve.wait_ge(ffn_hi, 1)
                        low_of(flat(ffn_w.lo), stage_a[:, 0:KT * FFN], flat(ffn_w.hi)).then_inc(ffn_lo, 1)
                    if c == 7 and attend and not back:
                        dve.wait_ge(w2_hi, 1)
                        low_of(flat(w2.lo), stage_b[:, :], flat(w2.hi)).then_inc(w2_lo, 1)
                        dve.wait_ge(b_hi, 2)
                        low_of(lora_b.lo[0:LR, :], stage_c[0:LR, 0, :], lora_b.hi[0:LR, :]).then_inc(b_lo, 1)
                        low_of(moe_b.lo[:, :], stage_c[:, 1, :], moe_b.hi[:, :]).then_inc(b_lo, 1)
                    if c == 1 and back:
                        dve.wait_ge(x1t_hi, r + 1)
                        low_of(flat(x1_t.lo), x_ps[:, :], flat(x1_t.hi)).then_inc(x1t_lo, 1)
                    if c == 2 and back:
                        dve.wait_ge(low_hi, r + 1)
                        nc.vector.scalar_tensor_tensor(low_t.lo[:, :], y_ps[:, 0:P], LORA_SCALE, f32(low_t.hi[:, :]),
                                                       ALU.mult, ALU.subtract).then_inc(low_lo, 1)
                    if c == 4 and back:
                        dve.wait_ge(c2t_hi, r + 1)
                        low_of(flat(c2_t.lo), x_ps[:, :], flat(c2_t.hi)).then_inc(c2t_lo, 1)
                    if c == 6 and back:
                        choose_experts(r)
                    if c == 7:
                        if back:
                            gate_hidden(r)
                        if front:
                            dve.wait_ge(ct_hi, f + 1)
                            low_of(flat(c_t.lo), y_ps[:, :], flat(c_t.hi)).then_inc(ct_lo, 1)

                for c in range(CHUNKS):
                    slot(c)
                if back:
                    dve.wait_ge(ht_hi, r + 1)
                    low_of(hidden_t.lo[:, :], scores_ps[0][:, 0:P], hidden_t.hi[:, :]).then_inc(ht_lo, 1)
                if front:
                    if not attend and front:
                        dve.wait_ge(sin_signed, 1)
                    rotate(f, attend)
                if back:
                    dve.wait_ge(ffn_done, r + 1)
                    dve.wait_ge(x1b_ready, r + 1)
                    dve.wait_ge(out_free, 16 * (r + 1))
                    nc.vector.tensor_tensor(out_sb[:, :], z_ps[:, :], x1_bias[:, :], ALU.add).then_inc(out_ready, 1)

            iterations(dve, iteration)

        @block.tensor
        def _(pe):
            def product(out, lhs, rhs, first, last):
                for n, (a, b) in enumerate((("hi", "hi"), ("lo", "hi"), ("hi", "lo"))):
                    mm = nc.tensor.matmul(out, lhs(a), rhs(b), start=first and n == 0, stop=last and n == 2)
                return mm

            half = lambda pair, name: pair.hi if name == "hi" else pair.lo

            def over_k(out, lhs_pair, rhs_pair, cols, last=True):
                for k in range(KT):
                    mm = product(out, lambda h: half(lhs_pair, h)[:, k, :], lambda h: half(rhs_pair, h)[:, k, cols],
                                 k == 0, last and k == KT - 1)
                return mm

            def transposes(out, tile):
                for k in range(KT):
                    mm = nc.tensor.transpose(out[:, k * P:(k + 1) * P], tile[:, k * P:(k + 1) * P], ident[:, :])
                return mm

            def score_chunk(t, c):
                p, e = c // 2, c % 2
                if c == 0:
                    pe.wait_ge(kd_hi, t + 1)
                    pe.wait_ge(kd_lo, t + 1)
                    pe.wait_ge(qt_hi, t + 1)
                    pe.wait_ge(qt_lo, t + 1)
                if c >= 2:
                    pe.wait_ge(exped, CHUNKS * t + c - 1)
                out = scores_ps[c % 2][:, :]
                product(out, lambda h: half(q_t, h)[:, p, :],
                        lambda h: half(k_diag, h)[:, e * PAIRS:(e + 1) * PAIRS, :], True, False)
                nc.tensor.matmul(out, ident_bf[:, :], causal[:, :, :], start=False, stop=True).then_inc(scored, 1)

            def transpose_probs(t, c):
                pe.wait_ge(exped, CHUNKS * t + c + 1)
                if c >= 2:
                    pe.wait_ge(pt_odd if c % 2 else pt_even, PER * t + c // 2)
                for j in range(PAIRS):
                    mm = nc.tensor.transpose(probs_t_ps[c % 2][:, j * P:(j + 1) * P], probs[c % 2][:, j, :],
                                             ident[:, :])
                mm.then_inc(pt_done, 1)

            def context_chunk(t, c):
                p, e = c // 2, c % 2
                if c == 0:
                    pe.wait_ge(v_ready, 2 * (t + 1))
                pe.wait_ge(pt_odd if c % 2 else pt_even, PER * t + c // 2 + 1)
                for j in range(PAIRS):
                    mm = nc.tensor.matmul(ctx_ps[2 * HD * j:2 * HD * (j + 1), p * P:(p + 1) * P],
                                          v_pad[e][:, j, :, :], probs_t[c % 2][:, j, :], start=(e == 0),
                                          stop=(e == 1))
                mm.then_inc(ctx_done, 1)

            def iteration(t, front, attend, back):
                f, r = t + 1, t - 1
                if attend and not back:
                    pe.wait_ge(tables_made, 5)
                if back:
                    pe.wait_ge(inv_ready, r + 1)
                    pe.wait_ge(pt_even, PER * (r + 1))
                    transposes(probs_t_ps[0], inv_wide).then_inc(inv_t_done, 1)
                if attend:
                    pe.wait_ge(qk_ready, t + 1)
                    pe.wait_ge(v_ready, 2 * (t + 1))
                    nc.tensor.transpose(y_ps[:, 0:P], qk[:, D:QK], ident[:, :]).then_inc(kt_done, 1)
                    transposes(x_ps, qk).then_inc(qt_done, 1)
                if back:
                    pe.wait_ge(o_lo, 1)
                    pe.wait_ge(ctx_hi, r + 1)
                    pe.wait_ge(ctx_lo, r + 1)
                    pe.wait_ge(pt_odd, PER * (r + 1))
                    over_k(probs_t_ps[1][:, :], ctx_t, o_w, slice(0, D)).then_inc(attn_done, 1)

                def slot(c):
                    if attend:
                        score_chunk(t, c)
                    if c == 1 and back:
                        pe.wait_ge(x1_ready, r + 1)
                        transposes(x_ps, x1).then_inc(x1t_done, 1)
                    if c == 2 and back:
                        pe.wait_ge(x1t_hi, r + 1)
                        pe.wait_ge(x1t_lo, r + 1)
                        pe.wait_ge(a_hi, r + 1)
                        pe.wait_ge(a_lo, r + 1)
                        over_k(y_ps[:, 0:P], lora_aw, x1_t, slice(0, P)).then_inc(low_done, 1)
                        pe.wait_ge(w2_lo, 1)
                        over_k(z_ps[:, :], x1_t, w2, slice(0, D), last=False)
                    if c == 3 and back:
                        pe.wait_ge(b_lo, 2)
                        pe.wait_ge(low_hi, r + 1)
                        pe.wait_ge(low_lo, r + 1)
                        product(z_ps[:, :], lambda h: half(low_t, h)[:, :], lambda h: half(lora_b, h)[:, :], False,
                                True).then_inc(c2_done, 1)
                    if c == 4 and back:
                        pe.wait_ge(c2_copied, r + 1)
                        transposes(x_ps, turn).then_inc(c2t_done, 1)
                    if c == 5 and front:
                        pe.wait_ge(xt_hi, f + 1)
                        pe.wait_ge(xt_lo, f + 1)
                        pe.wait_ge(cond_hi, KT * (f + 1))
                        pe.wait_ge(cond_lo, KT * (f + 1))
                        over_k(y_ps[:, :], xt, cond_w, slice(0, D)).then_inc(c_done, 1)
                    if c == 6 and back:
                        pe.wait_ge(ffn_lo, 1)
                        pe.wait_ge(c2t_hi, r + 1)
                        pe.wait_ge(c2t_lo, r + 1)
                        over_k(x_ps[:, 0:GATES], c2_t, ffn_w, slice(0, GATES)).then_inc(gates_done, 1)
                        over_k(z_ps[:, :], c2_t, ffn_w, slice(GATES, FFN), last=False)
                    if c == 7 and front:
                        pe.wait_ge(c_copied, f + 1)
                        if not attend and front:
                            pe.wait_ge(tables_made, 5)
                        transposes(y_ps, turn).then_inc(ct_done, 1)
                    if attend and c >= 1:
                        transpose_probs(t, c - 1)
                    if attend and c >= 2:
                        context_chunk(t, c - 2)

                for c in range(CHUNKS):
                    slot(c)
                if front:
                    if not attend and front:
                        pe.wait_ge(qkv_lo, 1)
                    pe.wait_ge(ct_hi, f + 1)
                    pe.wait_ge(ct_lo, f + 1)
                    if back:
                        pe.wait_ge(hidden_ready, 6 * (r + 1))
                    over_k(x_ps[:, :], c_t, qkv_w, slice(0, D))
                    over_k(y_ps[:, 0:2 * KV], c_t, qkv_w, slice(D, QKV)).then_inc(qkv_done, 1)
                if back:
                    pe.wait_ge(hidden_ready, 6 * (r + 1))
                    nc.tensor.transpose(scores_ps[0][:, 0:P], hidden[:, :], ident[:, :]).then_inc(ht_done, 1)
                if attend:
                    transpose_probs(t, CHUNKS - 1)
                    context_chunk(t, CHUNKS - 2)
                    context_chunk(t, CHUNKS - 1)
                if back:
                    pe.wait_ge(ht_hi, r + 1)
                    pe.wait_ge(ht_lo, r + 1)
                    product(z_ps[:, :], lambda h: half(hidden_t, h)[:, :], lambda h: half(moe_b, h)[:, :], False,
                            True).then_inc(ffn_done, 1)

            iterations(pe, iteration)


def kernel(x, itok_B_3_7, itok_B_0_2, L0_cond_weight, L0_attn_Wq, L0_attn_Wk, L0_attn_Wv, L0_attn_Wo, L0_attn_cos,
           L0_attn_sin, L0_cond2_W, L0_cond2_lora_A, L0_cond2_lora_B_w, L0_ffn_W_base, L0_ffn_b_base,
           L0_ffn_W_router, L0_ffn_A, L0_ffn_B):
    import numpy as np
    import concourse.bacc as bacc
    from concourse.bass_utils import run_bass_kernel_spmd

    lay = np.ascontiguousarray
    a = {k: np.asarray(v) for k, v in locals().items() if k[0] in "xiL"}
    D = a["x"].shape[2]
    HD = a["L0_attn_cos"].shape[1]
    KV = a["L0_attn_Wk"].shape[1]
    GROUPS, PER = KV // HD, D // KV
    experts, _, rank = a["L0_ffn_B"].shape

    arrays = {
        "x": lay(a["x"]),
        "x_t": lay(a["x"].transpose(0, 2, 1)),
        "cond_ids": lay(a["itok_B_3_7"]),
        "lora_ids": lay(a["itok_B_0_2"]),
        "cond_w_t": lay(a["L0_cond_weight"].transpose(0, 2, 1)),
        "w_q": lay(a["L0_attn_Wq"].reshape(D, GROUPS, PER, HD).transpose(0, 2, 1, 3).reshape(D, D)),
        "w_kv": lay(np.concatenate([a["L0_attn_Wk"], a["L0_attn_Wv"]], axis=1)),
        "w_o": lay(a["L0_attn_Wo"].reshape(GROUPS, PER, HD, D).transpose(1, 0, 2, 3).reshape(D, D)),
        "cos": lay(a["L0_attn_cos"]),
        "sin": lay(a["L0_attn_sin"]),
        "w2_t": lay(a["L0_cond2_W"].T),
        "lora_a": lay(a["L0_cond2_lora_A"]),
        "lora_b_t": lay(a["L0_cond2_lora_B_w"].T),
        "base_t": lay(a["L0_ffn_W_base"].T),
        "base_bias": lay(a["L0_ffn_b_base"]),
        "router_t": lay(a["L0_ffn_W_router"].T),
        "experts_a_t": lay(a["L0_ffn_A"].reshape(experts * rank, D).T),
        "experts_b": lay(a["L0_ffn_B"].transpose(0, 2, 1).reshape(experts * rank, D)),
    }
    nc = bacc.Bacc("TRN2", target_bir_lowering=False, num_devices=1)
    aps = {n: nc.dram_tensor(n, v.shape, mybir.dt.from_np(v.dtype), kind="ExternalInput").ap()
           for n, v in arrays.items()}
    out = nc.dram_tensor("out", a["x"].shape, F32, kind="ExternalOutput").ap()
    build_program(nc, **aps, out=out)
    r = run_bass_kernel_spmd(nc, [arrays], core_ids=[0])
    return r.results[0]["out"]
```

```python
from contextlib import ExitStack

import concourse.bass as bass
from concourse import mybir

ALU = mybir.AluOpType
ACT = mybir.ActivationFunctionType
AX_X = mybir.AxisListType.X
F32 = mybir.dt.float32
F32R = mybir.dt.float32r
BF16 = mybir.dt.bfloat16
U32 = mybir.dt.uint32
I32 = mybir.dt.int32

P = 128
MASKED = -3.0e38


def build_program(nc, x, x_t, cond_ids, lora_ids, cond_w_t, w_q, w_kv, w_o, cos, sin, w2_t, lora_a, lora_b_t,
                  base_t, base_bias, router_t, experts_a_t, experts_b, out):
    BATCH, T, D = x.shape
    assert T == P
    KT = D // P
    HD = cos.shape[1]
    KV = w_kv.shape[1] // 2
    GROUPS = KV // HD
    PER = D // KV
    HEADS = GROUPS * PER
    PAIRS = GROUPS // 2
    assert KV == P and 2 * HD == 32
    CHUNKS = 2 * PER
    EXPERTS = router_t.shape[1]
    RANK = experts_a_t.shape[1] // EXPERTS
    LR = lora_a.shape[2]
    GATES = EXPERTS + EXPERTS * RANK
    NCOND, NLORA = cond_w_t.shape[0], lora_a.shape[0]
    QK = D + KV
    QKV = D + 2 * KV
    FFN = GATES + D
    SCORE_SCALE = float(HD) ** -0.5
    LORA_SCALE = 16 / 32
    MOE_SCALE = 32 / 16

    with ExitStack() as ctx:
        def sb(name, shape, dt=F32):
            return ctx.enter_context(nc.sbuf_tensor(name, shape, dt))

        def sem(name):
            return ctx.enter_context(nc.semaphore(name))

        class Pair:

            def __init__(self, name, shape):
                self.hi, self.lo = sb(name + "_hi", shape, F32R), sb(name + "_lo", shape, F32R)

        bank = [ctx.enter_context(nc.psum_tensor(f"bank{i}", [P, 512], F32)) for i in range(8)]
        scores_ps = bank[0:2]
        probs_t_ps = bank[2]
        ctx_ps = bank[3]
        x_ps = bank[4]
        y_ps = bank[5]
        z_ps = bank[6]
        w_ps = bank[7]

        qkv_w = Pair("qkv_w", [P, KT, QKV])
        o_w = Pair("o_w", [P, KT, D])
        w2 = Pair("w2", [P, KT, D])
        ffn_w = Pair("ffn_w", [P, KT, FFN])
        lora_b = Pair("lora_b", [P, D])
        moe_b = Pair("moe_b", [P, D])
        stage_a = sb("stage_a", [P, KT * QKV])
        stage_b = sb("stage_b", [P, KT * D])
        spare = sb("spare", [P, 2, D])
        stage_c = spare
        cond_raw = sb("cond_raw", [P, KT, D])
        cond_w = Pair("cond_w", [P, KT, D])
        a_raw = sb("a_raw", [P, KT, LR])
        lora_aw = Pair("lora_aw", [P, KT, P])
        bias_row = sb("bias_row", [P, D])
        ids = sb("ids", [1, 2 * BATCH], I32)

        ident = sb("ident", [P, P])
        ident_bf = sb("ident_bf", [P, P], BF16)
        causal = sb("causal", [P, 4, P], BF16)
        own_group = sb("own_group", [P, GROUPS])
        rope_cos = sb("rope_cos", [P, HD])
        rope_sin = sb("rope_sin", [P, HD])
        expert_no = sb("expert_no", [P, EXPERTS])

        xt_raw = sb("xt_raw", [P, KT, P])
        xt = Pair("xt", [P, KT, P])
        x_nat = sb("x_nat", [P, D])
        turn = sb("turn", [P, D])
        c_t = Pair("c_t", [P, KT, P])
        rope_a = sb("rope_a", [P, QK])
        rope_b = sb("rope_b", [P, QK])
        qk = sb("qk", [P, QK])
        q_t = Pair("q_t", [P, PER, P])
        k_t = Pair("k_t", [P, P])
        k_diag = Pair("k_diag", [P, GROUPS, P])
        v_nat = sb("v_nat", [P, KV])
        v_pad = [sb(f"v_pad{e}", [P, PAIRS, 2, HD]) for e in range(2)]
        neg_max = sb("neg_max", [P, HEADS])
        sums = sb("sums", [P, HEADS])
        inv_sum = sb("inv_sum", [P, HEADS])
        probs = [sb(f"probs{i}", [P, PAIRS, P]) for i in range(2)]
        probs_t = [sb(f"probs_t{i}", [P, PAIRS, P]) for i in range(2)]
        inv_wide, ctx_n = spare[:, 0, :], spare[:, 1, :]
        inv_t = rope_a[:, 0:D]
        ctx_t = Pair("ctx_t", [P, PER, P])
        x1 = sb("x1", [P, D])
        x1_bias = sb("x1_bias", [P, D])
        x1_t = Pair("x1_t", [P, KT, P])
        low_t = Pair("low_t", [P, P])
        c2_t = Pair("c2_t", [P, KT, P])
        logits = sb("logits", [P, EXPERTS])
        top = sb("top", [P, 8])
        top_at = sb("top_at", [P, 8], U32)
        top_no = sb("top_no", [P, 2])
        neg_top = sb("neg_top", [P, 1])
        top_less = sb("top_less", [P, 2])
        top_exp = sb("top_exp", [P, 2])
        top_sum = sb("top_sum", [P, 1])
        top_inv = sb("top_inv", [P, 1])
        top_w = sb("top_w", [P, 2])
        pick = sb("pick", [P, 2, EXPERTS])
        gate = sb("gate", [P, EXPERTS])
        hidden = sb("hidden", [P, EXPERTS * RANK])
        hidden_t = Pair("hidden_t", [P, P])
        out_sb = sb("out_sb", [P, D])

        ids_in, tables_in, bias_in = sem("ids_in"), sem("tables_in"), sem("bias_in")
        cond_in, xt_in, x_in, a_in = sem("cond_in"), sem("xt_in"), sem("x_in"), sem("a_in")
        qkv_in, o_in, w2_in, ffn_in, b_in = sem("qkv_in"), sem("o_in"), sem("w2_in"), sem("ffn_in"), sem("b_in")
        out_free = sem("out_free")
        zeroed, tables_made, sin_signed = sem("zeroed"), sem("tables_made"), sem("sin_signed")
        qkv_hi, o_hi, w2_hi, ffn_hi, b_hi = sem("qkv_hi"), sem("o_hi"), sem("w2_hi"), sem("ffn_hi"), sem("b_hi")
        qkv_lo, o_lo, w2_lo, ffn_lo, b_lo = sem("qkv_lo"), sem("o_lo"), sem("w2_lo"), sem("ffn_lo"), sem("b_lo")
        cond_hi, cond_lo, xt_hi, xt_lo = sem("cond_hi"), sem("cond_lo"), sem("xt_hi"), sem("xt_lo")
        cond_lo_first = sem("cond_lo_first")
        a_hi, a_lo = sem("a_hi"), sem("a_lo")
        c_done, c_copied, ct_done, ct_hi, ct_lo = (sem("c_done"), sem("c_copied"), sem("ct_done"), sem("ct_hi"),
                                                   sem("ct_lo"))
        q_done, kv_done = sem("q_done"), sem("kv_done")
        rope_mul, v_copied, v_ready, qk_ready = sem("rope_mul"), sem("v_copied"), sem("v_ready"), sem("qk_ready")
        kt_done, qt_done, kt_hi, kt_lo = sem("kt_done"), sem("qt_done"), sem("kt_hi"), sem("kt_lo")
        kd_hi, kd_lo, qt_hi, qt_lo = sem("kd_hi"), sem("kd_lo"), sem("qt_hi"), sem("qt_lo")
        scored, maxed, exped, pt_done = sem("scored"), sem("maxed"), sem("exped"), sem("pt_done")
        pt_even, pt_odd, ctx_done = sem("pt_even"), sem("pt_odd"), sem("ctx_done")
        inverted, inv_ready, inv_t_done, inv_t_ready = (sem("inverted"), sem("inv_ready"), sem("inv_t_done"),
                                                        sem("inv_t_ready"))
        ctx_normed, ctx_hi, ctx_lo = sem("ctx_normed"), sem("ctx_hi"), sem("ctx_lo")
        attn_done, x1_ready, x1b_ready = sem("attn_done"), sem("x1_ready"), sem("x1b_ready")
        x1t_done, x1t_hi, x1t_lo = sem("x1t_done"), sem("x1t_hi"), sem("x1t_lo")
        low_done, low_hi, low_lo = sem("low_done"), sem("low_hi"), sem("low_lo")
        c2_done, c2_copied, c2t_done, c2t_hi, c2t_lo = (sem("c2_done"), sem("c2_copied"), sem("c2t_done"),
                                                        sem("c2t_hi"), sem("c2t_lo"))
        gates_done, gating, top_exped, hidden_ready = (sem("gates_done"), sem("gating"), sem("top_exped"),
                                                       sem("hidden_ready"))
        ht_done, ht_hi, ht_lo, ffn_done, out_ready = (sem("ht_done"), sem("ht_hi"), sem("ht_lo"), sem("ffn_done"),
                                                      sem("out_ready"))

        f32 = lambda ap: ap.bitcast(F32)
        flat = lambda t: t[:, :, :].rearrange("p a b -> p (a b)")

        def iterations(eng, iteration):
            iteration(-2, prep=True)
            iteration(-1, prep=True, front=True)
            iteration(0, prep=True, front=True, attend=True)
            iteration(1, prep=True, front=True, attend=True, back=True)
            with eng.Fori(2, BATCH - 2) as t:
                iteration(t, prep=True, front=True, attend=True, back=True, tail=True)
            iteration(BATCH - 2, front=True, attend=True, back=True, tail=True)
            iteration(BATCH - 1, attend=True, back=True, tail=True)
            iteration(BATCH, back=True, tail=True)
            iteration(BATCH + 1, tail=True)

        block = ctx.enter_context(nc.Block())

        @block.sync
        def _(sp):
            def iteration(t, prep=False, front=False, attend=False, back=False, tail=False):
                g, f, r = t + 2, t + 1, t - 1
                if prep:
                    n = sp.value_load(ids[0:1, bass.ds(g, 1)], min_val=0, max_val=NCOND - 1)
                    if front:
                        if attend:
                            sp.wait_ge(cond_lo, KT * (g - 1))
                        else:
                            sp.wait_ge(cond_lo_first, KT)
                        sp.wait_ge(xt_lo, g)
                        sp.wait_ge(ids_in, 32)
                    sp.dma_start(cond_raw[:, :, :],
                                 cond_w_t[bass.ds(n, 1), :, :].rearrange("a (k p) o -> p (a k) o", p=P)
                                 ).then_inc(cond_in, 16)
                    sp.dma_start(xt_raw[:, :, :], x_t[bass.ds(g, 1), :, :].rearrange("a (k p) s -> p (a k) s", p=P)
                                 ).then_inc(xt_in, 16)
                if prep and not front:
                    stage_qkv = stage_a[:, :].rearrange("p (k n) -> p k n", k=KT)
                    sp.dma_start(stage_qkv[:, :, 0:D], w_q.rearrange("(k p) n -> p k n", p=P)).then_inc(qkv_in, 16)
                    sp.dma_start(stage_qkv[:, :, D:QKV], w_kv.rearrange("(k p) n -> p k n", p=P)).then_inc(qkv_in, 16)
                    sp.dma_start(rope_cos[:, :], cos[0:P, :]).then_inc(tables_in, 16)
                    sp.dma_start(rope_sin[:, :], sin[0:P, :]).then_inc(tables_in, 16)
                if prep and not front:
                    stage_3 = stage_b[:, :].rearrange("p (k n) -> p k n", k=KT)
                    sp.dma_start(stage_3, w_o.rearrange("(k p) n -> p k n", p=P)).then_inc(o_in, 16)
                    sp.dma_start(bias_row[:, :], base_bias.partition_broadcast(P)).then_inc(bias_in, 16)
                    sp.dma_start(stage_c[0:LR, 0, :], lora_b_t).then_inc(b_in, 16)
                    sp.dma_start(stage_c[:, 1, :], experts_b).then_inc(b_in, 16)
                if front and not attend:
                    sp.wait_ge(qkv_lo, 1)
                    stage_ffn = stage_a[:, 0:KT * FFN].rearrange("p (k n) -> p k n", k=KT)
                    for src, at in ((router_t, 0), (experts_a_t, EXPERTS), (base_t, GATES)):
                        sp.dma_start(stage_ffn[:, :, at:at + src.shape[1]], src.rearrange("(k p) n -> p k n", p=P)
                                     ).then_inc(ffn_in, 16)
                    sp.wait_ge(o_lo, 1)
                    stage_3 = stage_b[:, :].rearrange("p (k n) -> p k n", k=KT)
                    sp.dma_start(stage_3, w2_t.rearrange("(k p) n -> p k n", p=P)).then_inc(w2_in, 16)
                if attend:
                    n = sp.value_load(ids[0:1, bass.ds(t + BATCH, 1)], min_val=0, max_val=NLORA - 1)
                    if back:
                        sp.wait_ge(x1_ready, t)
                        sp.wait_ge(a_lo, t)
                        sp.wait_ge(ids_in, 32)
                    sp.dma_start(x_nat[:, :], x[bass.ds(t, 1), :, :].rearrange("a s d -> s (a d)")).then_inc(x_in, 16)
                    sp.dma_start(a_raw[:, :, :], lora_a[bass.ds(n, 1), :, :].rearrange("a (k p) r -> p (a k) r", p=P)
                                 ).then_inc(a_in, 16)
                if tail:
                    sp.wait_ge(out_ready, t - 1)
                    sp.wait_ge(ids_in, 32)
                    sp.dma_start(out[bass.ds(t - 2, 1), :, :].rearrange("a s d -> s (a d)"), out_sb[:, :]
                                 ).then_inc(out_free, 16)

            sp.dma_start(ids[0:1, 0:BATCH], cond_ids.rearrange("(a n) -> a n", a=1)).then_inc(ids_in, 16)
            sp.dma_start(ids[0:1, BATCH:2 * BATCH], lora_ids.rearrange("(a n) -> a n", a=1)).then_inc(ids_in, 16)
            sp.wait_ge(ids_in, 32)
            iterations(sp, iteration)
            sp.wait_ge(out_free, 16 * (BATCH + 1))

        @block.gpsimd
        def _(pool):
            def tables():
                pool.memset(ident[:, :], 0.0).then_inc(zeroed, 1)
                pool.memset(ident_bf[:, :], 0.0).then_inc(zeroed, 1)
                pool.memset(causal[:, :, :], 0.0).then_inc(zeroed, 1)
                pool.memset(own_group[:, :], 1.0).then_inc(zeroed, 1)
                pool.wait_ge(zeroed, 4)
                for tile in (ident, ident_bf):
                    pool.affine_select(out=tile[:, :], in_=tile[:, :], compare_op=ALU.not_equal, fill=1.0, base=0,
                                       pattern=[[-1, P]], channel_multiplier=1).then_inc(tables_made, 1)
                pool.affine_select(out=causal[:, :, :], in_=causal[:, :, :], compare_op=ALU.is_ge, fill=MASKED,
                                   base=0, pattern=[[0, 4], [-1, P]], channel_multiplier=1).then_inc(tables_made, 1)
                grp = own_group[:, :].rearrange("p (e j) -> p e j", e=2)
                pool.affine_select(out=grp, in_=grp, compare_op=ALU.is_ge, fill=0.0, base=0,
                                   pattern=[[-HD, 2], [-2 * HD, PAIRS]], channel_multiplier=1
                                   ).then_inc(tables_made, 1)
                pool.wait_ge(tables_made, 4)
                pool.affine_select(out=grp, in_=grp, compare_op=ALU.is_ge, fill=0.0, base=HD - 1,
                                   pattern=[[HD, 2], [2 * HD, PAIRS]], channel_multiplier=-1
                                   ).then_inc(tables_made, 1)

            def clear():
                for e in range(2):
                    pool.memset(v_pad[e][:, :, :, :], 0.0).then_inc(zeroed, 1)
                for half in (lora_b.hi, lora_b.lo):
                    pool.memset(half[:, :].bitcast(F32), 0.0).then_inc(zeroed, 1)
                for half in (lora_aw.hi, lora_aw.lo):
                    pool.memset(half[:, :, :].bitcast(F32), 0.0).then_inc(zeroed, 1)
                pool.iota(expert_no[:, :], [[1, EXPERTS]], base=0, channel_multiplier=0,
                          allow_small_or_imprecise_dtypes=True).then_inc(zeroed, 1)
                pool.memset(out_sb[:, :], 0.0).then_inc(out_free, 16)

            def spread_k_low(f, e, again):
                if e == 0:
                    pool.wait_ge(kt_lo, f + 1)
                if again:
                    pool.wait_ge(scored, CHUNKS * f - 1 + e)
                pool.tensor_tensor(k_diag.lo[:, e * PAIRS:(e + 1) * PAIRS, :],
                                   f32(k_t.lo[:, :]).unsqueeze(1).broadcast_to([P, PAIRS, P]),
                                   own_group[:, e * PAIRS:(e + 1) * PAIRS].unsqueeze(2).broadcast_to([P, PAIRS, P]),
                                   ALU.mult).then_inc(kd_lo, 1)

            def iteration(t, prep=False, front=False, attend=False, back=False, tail=False):
                g, f, r = t + 2, t + 1, t - 1

                def split_cond(k):
                    pool.wait_ge(cond_hi, KT * g + k + 1)
                    pool.tensor_tensor(cond_w.lo[:, k, :], cond_raw[:, k, :], f32(cond_w.hi[:, k, :]), ALU.subtract
                                       ).then_inc(cond_lo, 1)

                if back:
                    pool.wait_ge(a_hi, r + 1)
                    pool.tensor_tensor(lora_aw.lo[:, :, 0:LR], a_raw[:, :, :], f32(lora_aw.hi[:, :, 0:LR]),
                                       ALU.subtract).then_inc(a_lo, 1)
                if prep and not front:
                    clear()
                if prep:
                    pool.wait_ge(xt_hi, g + 1)
                    pool.tensor_tensor(xt.lo[:, :, :], xt_raw[:, :, :], f32(xt.hi[:, :, :]), ALU.subtract
                                       ).then_inc(xt_lo, 1)
                if prep and front:
                    split_cond(0)
                    split_cond(1)
                if back:
                    pool.wait_ge(bias_in, 16)
                    pool.wait_ge(x1_ready, r + 1)
                    if tail:
                        pool.wait_ge(out_ready, t - 1)
                    pool.tensor_tensor(x1_bias[:, :], x1[:, :], bias_row[:, :], ALU.add).then_inc(x1b_ready, 1)
                if prep and front:
                    split_cond(2)
                if front:
                    for n, (at, w) in enumerate(((0, D), (D, KV))):
                        pool.wait_ge(rope_mul, 2 * f + n + 1)
                        pool.tensor_tensor(qk[:, at:at + w], rope_a[:, at:at + w], rope_b[:, at:at + w], ALU.add
                                           ).then_inc(qk_ready, 1)
                if prep and front:
                    split_cond(3)
                if front:
                    for e in range(2):
                        spread_k_low(f, e, attend)
                if attend and not back:
                    pool.wait_ge(w2_hi, 1)
                    pool.tensor_tensor(flat(w2.lo), stage_b[:, :], f32(flat(w2.hi)), ALU.subtract).then_inc(w2_lo, 1)

            tables()
            iterations(pool, iteration)

        @block.scalar
        def _(act):
            def copy(out, in_, scale=1.0):
                return nc.scalar.activation(out, in_, ACT.Copy, scale=scale)

            def exp_chunk(t, c, again):
                act.wait_ge(maxed, CHUNKS * t + c + 1)
                if c >= 2 or again:
                    act.wait_ge(pt_done, CHUNKS * t + c - 1)
                p, e = c // 2, c % 2
                for j in range(PAIRS):
                    h = p * GROUPS + 2 * j + e
                    last = nc.scalar.activation(probs[c % 2][:, j, :], scores_ps[c % 2][:, j * P:(j + 1) * P],
                                                ACT.Exp, bias=neg_max[:, h:h + 1], accum_out=sums[:, h:h + 1])
                last.then_inc(exped, 1)

            def evacuate_odd(b, c, again):
                act.wait_ge(pt_done, CHUNKS * b + c + 1)
                if c >= 2 or again:
                    act.wait_ge(ctx_done, CHUNKS * b + c - 1)
                copy(flat(probs_t[1]), probs_t_ps[:, :]).then_inc(pt_odd, 1)

            def iteration(t, prep=False, front=False, attend=False, back=False, tail=False):
                g, f, r = t + 2, t + 1, t - 1

                def split_cond(k):
                    act.wait_ge(cond_in, 16 * (g + 1))
                    copy(cond_w.hi[:, k, :], cond_raw[:, k, :]).then_inc(cond_hi, 1)

                for c in range(CHUNKS):
                    if c == 5 and back:
                        act.wait_ge(low_done, r + 1)
                        copy(low_t.hi[:, :], x_ps[:, 0:P], LORA_SCALE).then_inc(low_hi, 1)
                    if c == 4 and back:
                        act.wait_ge(x1t_done, r + 1)
                        copy(flat(x1_t.hi), x_ps[:, :]).then_inc(x1t_hi, 1)
                    if c == 1 and tail:
                        act.wait_ge(ht_done, t - 1)
                        copy(hidden_t.hi[:, :], w_ps[:, 0:P]).then_inc(ht_hi, 1)
                    if c == 1 and back:
                        act.wait_ge(inv_t_done, r + 1)
                        copy(inv_t, x_ps[:, :]).then_inc(inv_t_ready, 1)
                    if attend:
                        if c == 0 and back:
                            act.wait_ge(inverted, t)
                        exp_chunk(t, c, back)
                    if c == 0 and back:
                        evacuate_odd(r, CHUNKS - 1, True)
                        act.wait_ge(a_in, 16 * (r + 1))
                        copy(lora_aw.hi[:, :, 0:LR], a_raw[:, :, :]).then_inc(a_hi, 1)
                    if c == 1 and front:
                        act.wait_ge(c_done, f + 1)
                        copy(turn[:, :], y_ps[:, :]).then_inc(c_copied, 1)
                    if c == 6 and back:
                        act.wait_ge(c2_done, r + 1)
                        copy(turn[:, :], z_ps[:, :]).then_inc(c2_copied, 1)
                    if attend and c in (2, 4, 6):
                        evacuate_odd(t, c - 1, back)
                    if c == 2 and front:
                        act.wait_ge(ct_done, f + 1)
                        copy(flat(c_t.hi), y_ps[:, :]).then_inc(ct_hi, 1)
                    if c == 2 and prep:
                        act.wait_ge(xt_in, 16 * (g + 1))
                        copy(flat(xt.hi), flat(xt_raw)).then_inc(xt_hi, 1)
                    if c in (3, 4, 5) and prep:
                        split_cond(c - 3)
                    if c == 5 and prep:
                        split_cond(3)
                    if c == 5 and prep and not front:
                        act.wait_ge(qkv_in, 32)
                        copy(flat(qkv_w.hi), stage_a[:, :]).then_inc(qkv_hi, 1)
                        act.wait_ge(o_in, 16)
                        copy(flat(o_w.hi), stage_b[:, :]).then_inc(o_hi, 1)
                    if c == 5 and front and not attend:
                        act.wait_ge(ffn_in, 48)
                        copy(flat(ffn_w.hi), stage_a[:, 0:KT * FFN]).then_inc(ffn_hi, 1)
                        act.wait_ge(b_in, 32)
                        act.wait_ge(zeroed, 11)
                        copy(lora_b.hi[0:LR, :], stage_c[0:LR, 0, :]).then_inc(b_hi, 1)
                        copy(moe_b.hi[:, :], stage_c[:, 1, :]).then_inc(b_hi, 1)
                    if c == 5 and attend and not back:
                        act.wait_ge(w2_in, 16)
                        copy(flat(w2.hi), stage_b[:, :]).then_inc(w2_hi, 1)
                    if c == 6 and back:
                        act.wait_ge(c2t_done, r + 1)
                        copy(flat(c2_t.hi), x_ps[:, :]).then_inc(c2t_hi, 1)
                    if c == 6 and front:
                        act.wait_ge(kt_done, f + 1)
                        if attend:
                            act.wait_ge(kd_lo, 2 * f)
                        copy(k_t.hi[:, :], w_ps[:, 0:P]).then_inc(kt_hi, 1)
                        act.wait_ge(qt_done, f + 1)
                        copy(q_t.hi[:, 0:PER - 1, :], y_ps[:, 0:(PER - 1) * P].rearrange("a (b c) -> a b c", c=P),
                             SCORE_SCALE).then_inc(qt_hi, 1)
                    if c == 7 and front:
                        if attend:
                            act.wait_ge(scored, CHUNKS * f)
                        act.wait_ge(qt_lo, 2 * f + 1)
                        copy(q_t.hi[:, PER - 1, :], y_ps[:, (PER - 1) * P:], SCORE_SCALE).then_inc(qt_hi, 1)
                    if c == 7 and back:
                        act.wait_ge(gating, 6 * r + 4)
                        nc.scalar.activation(top_exp[:, :], top_less[:, :], ACT.Exp).then_inc(top_exped, 1)

            iterations(act, iteration)

        @block.vector
        def _(dve):
            def low_of(pair_lo, value, pair_hi):
                return nc.vector.tensor_tensor(pair_lo, value, f32(pair_hi), ALU.subtract)

            def max_chunk(t, c):
                dve.wait_ge(scored, CHUNKS * t + c + 1)
                p, e = c // 2, c % 2
                heads = neg_max[:, p * GROUPS:(p + 1) * GROUPS].rearrange("q (j e) -> q e j", e=2)[:, e, :]
                nc.vector.tensor_reduce(heads, scores_ps[c % 2][:, :].rearrange("q (j s) -> q j s", s=P), AX_X,
                                        ALU.max, negate=True).then_inc(maxed, 1)

            def evacuate_even(t, c, again):
                dve.wait_ge(pt_done, CHUNKS * t + c + 1)
                if c >= 2 or again:
                    dve.wait_ge(ctx_done, CHUNKS * t + c - 1)
                nc.vector.tensor_copy(flat(probs_t[0]), probs_t_ps[:, :]).then_inc(pt_even, 1)

            def rotate(src, at, n):
                half = HD // 2
                head = lambda tile, at: tile[:, at:at + n * HD].rearrange("s (h d) -> s h d", d=HD)
                tab = lambda tile, lo, w: tile[:, lo:lo + w].unsqueeze(1).broadcast_to([P, n, w])
                nc.vector.tensor_tensor(head(rope_a, at), head(src, 0), tab(rope_cos, 0, HD), ALU.mult)
                for to, frm in ((0, half), (half, 0)):
                    last = nc.vector.tensor_tensor(head(rope_b, at)[:, :, to:to + half],
                                                   head(src, 0)[:, :, frm:frm + half],
                                                   tab(rope_sin, to, half), ALU.mult)
                return last

            def invert(r):
                dve.wait_ge(exped, CHUNKS * (r + 1))
                nc.vector.reciprocal(inv_sum[:, :], sums[:, :]).then_inc(inverted, 1)
                dve.wait_ge(b_lo, 2)
                dve.wait_ge(inverted, r + 1)
                nc.vector.tensor_copy(inv_wide.rearrange("s (h d) -> s h d", d=HD),
                                      inv_sum[:, :].unsqueeze(2).broadcast_to([P, HEADS, HD])).then_inc(inv_ready, 1)

            def spread_k_high(f, e, again):
                if again:
                    dve.wait_ge(scored, CHUNKS * f - 1 + e)
                nc.vector.tensor_tensor(k_diag.hi[:, e * PAIRS:(e + 1) * PAIRS, :],
                                        w_ps[:, 0:P].unsqueeze(1).broadcast_to([P, PAIRS, P]),
                                        own_group[:, e * PAIRS:(e + 1) * PAIRS].unsqueeze(2).broadcast_to(
                                            [P, PAIRS, P]), ALU.mult).then_inc(kd_hi, 1)

            def q_low(p0, p1):
                nc.vector.scalar_tensor_tensor(q_t.lo[:, p0:p1, :].rearrange("a b c -> a (b c)"),
                                               y_ps[:, p0 * P:p1 * P], SCORE_SCALE,
                                               f32(q_t.hi[:, p0:p1, :].rearrange("a b c -> a (b c)")), ALU.mult,
                                               ALU.subtract).then_inc(qt_lo, 1)

            def normalise(r):
                dve.wait_ge(inv_t_ready, r + 1)
                dve.wait_ge(ctx_done, CHUNKS * (r + 1))
                nc.vector.tensor_tensor(ctx_n, ctx_ps[:, :], inv_t, ALU.mult).then_inc(ctx_normed, 1)

            def split_context(r):
                dve.wait_ge(ctx_normed, r + 1)
                nc.vector.tensor_copy(flat(ctx_t.hi), ctx_n).then_inc(ctx_hi, 1)
                dve.wait_ge(ctx_hi, r + 1)
                low_of(flat(ctx_t.lo), ctx_n, flat(ctx_t.hi)).then_inc(ctx_lo, 1)

            def pad_v(t, again):
                if again:
                    dve.wait_ge(ctx_done, CHUNKS * t)
                else:
                    dve.wait_ge(zeroed, 11)
                dve.wait_ge(v_copied, t + 1)
                v = v_nat[:, :].rearrange("s (j e d) -> s j e d", e=2, d=HD)
                for e in range(2):
                    nc.vector.tensor_copy(v_pad[e][:, :, e, :], v[:, :, e, :]).then_inc(v_ready, 1)

            def choose_experts(r):
                n = 6 * r
                dve.wait_ge(gates_done, r + 1)
                nc.vector.tensor_copy(logits[:, :], x_ps[:, 0:EXPERTS]).then_inc(gating, 1)
                dve.wait_ge(gating, n + 1)
                nc.vector.tensor_reduce(neg_top[:, :], logits[:, :], AX_X, ALU.max, negate=True).then_inc(gating, 1)
                nc.vector.max(top[:, :], logits[:, :]).then_inc(gating, 1)
                dve.wait_ge(gating, n + 3)
                nc.vector.tensor_scalar(top_less[:, :], top[:, 0:2], neg_top[:, 0:1], None, ALU.add
                                        ).then_inc(gating, 1)
                nc.vector.max_index(top_at[:, :], top[:, :], logits[:, :]).then_inc(gating, 1)
                dve.wait_ge(gating, n + 5)
                nc.vector.tensor_copy(top_no[:, :], top_at[:, 0:2]).then_inc(gating, 1)

            def gate_hidden(r):
                n = 6 * r
                dve.wait_ge(top_exped, r + 1)
                nc.vector.tensor_reduce(top_sum[:, :], top_exp[:, :], AX_X, ALU.add).then_inc(hidden_ready, 1)
                dve.wait_ge(hidden_ready, n + 1)
                nc.vector.reciprocal(top_inv[:, :], top_sum[:, :]).then_inc(hidden_ready, 1)
                dve.wait_ge(hidden_ready, n + 2)
                nc.vector.tensor_scalar(top_w[:, :], top_exp[:, :], top_inv[:, 0:1], MOE_SCALE, ALU.mult, ALU.mult
                                        ).then_inc(hidden_ready, 1)
                dve.wait_ge(hidden_ready, n + 3)
                dve.wait_ge(gating, n + 6)
                for i in range(2):
                    last = nc.vector.tensor_scalar(pick[:, i, :], expert_no[:, :], top_no[:, i:i + 1],
                                                   top_w[:, i:i + 1], ALU.is_equal, ALU.mult)
                last.then_inc(hidden_ready, 1)
                dve.wait_ge(hidden_ready, n + 4)
                nc.vector.tensor_tensor(gate[:, :], pick[:, 0, :], pick[:, 1, :], ALU.add).then_inc(hidden_ready, 1)
                dve.wait_ge(hidden_ready, n + 5)
                nc.vector.tensor_tensor(hidden[:, :].rearrange("s (e n) -> s e n", n=RANK),
                                        x_ps[:, EXPERTS:GATES].rearrange("s (e n) -> s e n", n=RANK),
                                        gate[:, :].unsqueeze(2).broadcast_to([P, EXPERTS, RANK]), ALU.mult
                                        ).then_inc(hidden_ready, 1)

            def iteration(t, prep=False, front=False, attend=False, back=False, tail=False):
                f, r = t + 1, t - 1
                if prep and not front:
                    for k in range(KT):
                        dve.wait_ge(cond_hi, k + 1)
                        low_of(cond_w.lo[:, k, :], cond_raw[:, k, :], cond_w.hi[:, k, :]).then_inc(cond_lo_first, 1)
                    dve.wait_ge(qkv_hi, 1)
                    low_of(flat(qkv_w.lo), stage_a[:, :], flat(qkv_w.hi)).then_inc(qkv_lo, 1)
                    dve.wait_ge(tables_in, 32)
                    nc.vector.tensor_scalar(rope_sin[:, 0:HD // 2], rope_sin[:, 0:HD // 2], -1.0, None, ALU.mult
                                            ).then_inc(sin_signed, 1)
                    dve.wait_ge(o_hi, 1)
                    low_of(flat(o_w.lo), stage_b[:, :], flat(o_w.hi)).then_inc(o_lo, 1)
                if attend and not back:
                    dve.wait_ge(zeroed, 11)
                for c in range(CHUNKS):
                    if c == 1 and tail:
                        dve.wait_ge(ht_hi, t - 1)
                        low_of(hidden_t.lo[:, :], w_ps[:, 0:P], hidden_t.hi[:, :]).then_inc(ht_lo, 1)
                    if c == 2:
                        if back:
                            normalise(r)
                        if attend:
                            pad_v(t, back)
                        if back:
                            split_context(r)
                    if c == 2 and tail:
                        dve.wait_ge(ffn_done, t - 1)
                        dve.wait_ge(x1b_ready, t - 1)
                        dve.wait_ge(out_free, 16 * (t - 1))
                        nc.vector.tensor_tensor(out_sb[:, :], z_ps[:, :], x1_bias[:, :], ALU.add
                                                ).then_inc(out_ready, 1)
                    if c == 3 and front:
                        dve.wait_ge(ct_hi, f + 1)
                        low_of(flat(c_t.lo), y_ps[:, :], flat(c_t.hi)).then_inc(ct_lo, 1)
                    if c == 3 and back:
                        dve.wait_ge(attn_done, r + 1)
                        dve.wait_ge(x_in, 16 * (r + 1))
                        nc.vector.tensor_tensor(x1[:, :], z_ps[:, :], x_nat[:, :], ALU.add).then_inc(x1_ready, 1)
                    if c == 4 and back:
                        dve.wait_ge(x1t_hi, r + 1)
                        low_of(flat(x1_t.lo), x_ps[:, :], flat(x1_t.hi)).then_inc(x1t_lo, 1)
                    if c == 5 and back:
                        dve.wait_ge(low_hi, r + 1)
                        nc.vector.scalar_tensor_tensor(low_t.lo[:, :], x_ps[:, 0:P], LORA_SCALE, f32(low_t.hi[:, :]),
                                                       ALU.mult, ALU.subtract).then_inc(low_lo, 1)
                    if c == 7 and back:
                        dve.wait_ge(c2t_hi, r + 1)
                        low_of(flat(c2_t.lo), x_ps[:, :], flat(c2_t.hi)).then_inc(c2t_lo, 1)
                    if c == 7 and front:
                        dve.wait_ge(kt_hi, f + 1)
                        nc.vector.tensor_tensor(k_t.lo[:, :], w_ps[:, 0:P], f32(k_t.hi[:, :]), ALU.subtract
                                                ).then_inc(kt_lo, 1)
                        spread_k_high(f, 0, attend)
                    if attend:
                        max_chunk(t, c)
                    if c == 0 and back:
                        invert(r)
                    if c == 0 and tail:
                        gate_hidden(t - 2)
                    if attend and c % 2 == 1:
                        evacuate_even(t, c - 1, back)
                    if c == 4 and front:
                        dve.wait_ge(q_done, f + 1)
                        if attend:
                            dve.wait_ge(qk_ready, 2 * f)
                        else:
                            dve.wait_ge(sin_signed, 1)
                        rotate(y_ps, 0, HEADS).then_inc(rope_mul, 1)
                    if c == 5 and front:
                        dve.wait_ge(kv_done, f + 1)
                        rotate(w_ps, D, GROUPS).then_inc(rope_mul, 1)
                        nc.vector.tensor_copy(v_nat[:, :], w_ps[:, KV:2 * KV]).then_inc(v_copied, 1)
                    if c == 7 and front:
                        dve.wait_ge(qt_hi, 2 * f + 1)
                        q_low(0, PER - 1)
                        spread_k_high(f, 1, attend)
                        dve.wait_ge(qt_hi, 2 * f + 2)
                        q_low(PER - 1, PER)
                    if c == 7 and back:
                        choose_experts(r)
                    if attend and not back:
                        if c == 2:
                            dve.wait_ge(b_hi, 2)
                            low_of(lora_b.lo[0:LR, :], stage_c[0:LR, 0, :], lora_b.hi[0:LR, :]).then_inc(b_lo, 1)
                            low_of(moe_b.lo[:, :], stage_c[:, 1, :], moe_b.hi[:, :]).then_inc(b_lo, 1)
                            dve.wait_ge(ffn_hi, 1)
                        if c in (3, 4, 5, 6):
                            k = c - 3
                            raw = stage_a[:, 0:KT * FFN].rearrange("p (k n) -> p k n", k=KT)
                            low_of(ffn_w.lo[:, k, :], raw[:, k, :], ffn_w.hi[:, k, :]).then_inc(ffn_lo, 1)

            iterations(dve, iteration)

        @block.tensor
        def _(pe):
            half = lambda pair, name: pair.hi if name == "hi" else pair.lo

            def product(out, lhs, rhs, first, last):
                for n, (a, b) in enumerate((("hi", "hi"), ("lo", "hi"), ("hi", "lo"))):
                    mm = nc.tensor.matmul(out, lhs(a), rhs(b), start=first and n == 0, stop=last and n == 2)
                return mm

            def over_k(out, lhs_pair, rhs_pair, cols, last=True, ks=range(KT)):
                for k in ks:
                    mm = product(out, lambda h: half(lhs_pair, h)[:, k, :], lambda h: half(rhs_pair, h)[:, k, cols],
                                 k == 0, last and k == KT - 1)
                return mm

            def transposes(out, tile):
                for k in range(KT):
                    mm = nc.tensor.transpose(out[:, k * P:(k + 1) * P], tile[:, k * P:(k + 1) * P], ident[:, :])
                return mm

            def score_chunk(t, c, again):
                p, e = c // 2, c % 2
                if c < 2:
                    pe.wait_ge(kd_hi, 2 * t + c + 1)
                    pe.wait_ge(kd_lo, 2 * t + c + 1)
                if c == 0:
                    pe.wait_ge(qt_hi, 2 * t + 1)
                    pe.wait_ge(qt_lo, 2 * t + 1)
                if c == CHUNKS - 2:
                    pe.wait_ge(qt_hi, 2 * t + 2)
                    pe.wait_ge(qt_lo, 2 * t + 2)
                if c >= 2 or again:
                    pe.wait_ge(exped, CHUNKS * t + c - 1)
                out = scores_ps[c % 2][:, :]
                product(out, lambda h: half(q_t, h)[:, p, :],
                        lambda h: half(k_diag, h)[:, e * PAIRS:(e + 1) * PAIRS, :], True, False)
                nc.tensor.matmul(out, ident_bf[:, :], causal[:, :, :], start=False, stop=True).then_inc(scored, 1)

            def transpose_probs(b, c, again):
                pe.wait_ge(exped, CHUNKS * b + c + 1)
                if c >= 1:
                    pe.wait_ge(pt_even if c % 2 else pt_odd, PER * b + (c + 1) // 2)
                elif again:
                    pe.wait_ge(pt_odd, PER * b)
                for j in range(PAIRS):
                    mm = nc.tensor.transpose(probs_t_ps[:, j * P:(j + 1) * P], probs[c % 2][:, j, :], ident[:, :])
                mm.then_inc(pt_done, 1)

            def context_chunk(b, c):
                p, e = c // 2, c % 2
                if c == 0:
                    pe.wait_ge(v_ready, 2 * (b + 1))
                pe.wait_ge(pt_odd if c % 2 else pt_even, PER * b + c // 2 + 1)
                for j in range(PAIRS):
                    mm = nc.tensor.matmul(ctx_ps[2 * HD * j:2 * HD * (j + 1), p * P:(p + 1) * P],
                                          v_pad[e][:, j, :, :], probs_t[c % 2][:, j, :], start=(e == 0),
                                          stop=(e == 1))
                mm.then_inc(ctx_done, 1)

            first_half, second_half = range(KT // 2), range(KT // 2, KT)

            def condition(f, attend, ks):
                if ks is first_half:
                    pe.wait_ge(xt_hi, f + 1)
                    pe.wait_ge(xt_lo, f + 1)
                    pe.wait_ge(cond_hi, KT * (f + 1))
                    if attend:
                        pe.wait_ge(cond_lo, KT * f)
                        pe.wait_ge(qt_lo, 2 * f)
                    else:
                        pe.wait_ge(cond_lo_first, KT)
                mm = over_k(y_ps[:, :], xt, cond_w, slice(0, D), ks=ks)
                if ks is second_half:
                    mm.then_inc(c_done, 1)

            def transpose_c(f, attend):
                pe.wait_ge(c_copied, f + 1)
                if not attend:
                    pe.wait_ge(tables_made, 5)
                transposes(y_ps, turn).then_inc(ct_done, 1)

            def project_q(f, attend):
                if not attend:
                    pe.wait_ge(qkv_lo, 1)
                pe.wait_ge(ct_hi, f + 1)
                pe.wait_ge(ct_lo, f + 1)
                over_k(y_ps[:, :], c_t, qkv_w, slice(0, D)).then_inc(q_done, 1)

            def project_kv(f, attend):
                if attend:
                    pe.wait_ge(kd_hi, 2 * f)
                over_k(w_ps[:, 0:2 * KV], c_t, qkv_w, slice(D, QKV)).then_inc(kv_done, 1)

            def transpose_qk(f):
                pe.wait_ge(qk_ready, 2 * (f + 1))
                pe.wait_ge(v_copied, f + 1)
                nc.tensor.transpose(w_ps[:, 0:P], qk[:, D:QK], ident[:, :]).then_inc(kt_done, 1)
                transposes(y_ps, qk).then_inc(qt_done, 1)

            def transpose_inverse(r):
                pe.wait_ge(inv_ready, r + 1)
                transposes(x_ps, inv_wide).then_inc(inv_t_done, 1)

            def project_out(r, tail):
                pe.wait_ge(o_lo, 1)
                if tail:
                    pe.wait_ge(out_ready, r)
                pe.wait_ge(ctx_hi, r + 1)
                pe.wait_ge(ctx_lo, r + 1)
                over_k(z_ps[:, :], ctx_t, o_w, slice(0, D)).then_inc(attn_done, 1)

            def transpose_x1(r):
                pe.wait_ge(x1_ready, r + 1)
                transposes(x_ps, x1).then_inc(x1t_done, 1)

            def project_low(r):
                pe.wait_ge(x1t_hi, r + 1)
                pe.wait_ge(x1t_lo, r + 1)
                pe.wait_ge(a_lo, r + 1)
                over_k(x_ps[:, 0:P], lora_aw, x1_t, slice(0, P)).then_inc(low_done, 1)

            def condition_2(r, ks):
                if ks is first_half:
                    pe.wait_ge(w2_lo, 1)
                over_k(z_ps[:, :], x1_t, w2, slice(0, D), last=False, ks=ks)
                if ks is second_half:
                    pe.wait_ge(b_lo, 2)
                    pe.wait_ge(low_hi, r + 1)
                    pe.wait_ge(low_lo, r + 1)
                    product(z_ps[:, :], lambda h: half(low_t, h)[:, :], lambda h: half(lora_b, h)[:, :], False,
                            True).then_inc(c2_done, 1)

            def transpose_c2(r):
                pe.wait_ge(c2_copied, r + 1)
                transposes(x_ps, turn).then_inc(c2t_done, 1)

            def gates(r):
                pe.wait_ge(ffn_lo, KT)
                pe.wait_ge(c2t_hi, r + 1)
                pe.wait_ge(c2t_lo, r + 1)
                over_k(x_ps[:, 0:GATES], c2_t, ffn_w, slice(0, GATES)).then_inc(gates_done, 1)

            def ffn_base(ks):
                over_k(z_ps[:, :], c2_t, ffn_w, slice(GATES, FFN), last=False, ks=ks)

            def transpose_hidden(q):
                pe.wait_ge(hidden_ready, 6 * (q + 1))
                nc.tensor.transpose(w_ps[:, 0:P], hidden[:, :], ident[:, :]).then_inc(ht_done, 1)

            def finish_ffn(q):
                pe.wait_ge(ht_hi, q + 1)
                pe.wait_ge(ht_lo, q + 1)
                product(z_ps[:, :], lambda h: half(hidden_t, h)[:, :], lambda h: half(moe_b, h)[:, :], False, True
                        ).then_inc(ffn_done, 1)

            def dense(t, c, front, attend, back, tail):
                f, r, q = t + 1, t - 1, t - 2
                if c == 0 and front:
                    condition(f, attend, first_half)
                if c == 0 and tail:
                    ffn_base(second_half)
                    transpose_hidden(q)
                if c == 0 and back:
                    transpose_inverse(r)
                if c == 1 and tail:
                    finish_ffn(q)
                if c == 2 and back:
                    project_out(r, tail)
                if c == 3 and front:
                    project_q(f, attend)
                if c == 3 and back:
                    transpose_x1(r)
                if c == 4 and front:
                    project_kv(f, attend)
                if c == 4 and back:
                    project_low(r)
                if c == 5 and back:
                    condition_2(r, first_half)
                if c == 6 and back:
                    transpose_c2(r)
                if c == 6 and front:
                    transpose_qk(f)
                if c == 7 and back:
                    gates(r)
                    ffn_base(first_half)

            def iteration(t, prep=False, front=False, attend=False, back=False, tail=False):
                f, r = t + 1, t - 1
                if attend and not back:
                    pe.wait_ge(tables_made, 5)
                for c in range(CHUNKS):
                    if attend:
                        score_chunk(t, c, back)
                    if c == 1 and front:
                        condition(f, attend, second_half)
                    if c == 6 and back:
                        condition_2(r, second_half)
                    if c == 0 and back:
                        transpose_probs(r, CHUNKS - 1, True)
                        context_chunk(r, CHUNKS - 2)
                    if attend and c >= 1:
                        transpose_probs(t, c - 1, back)
                    if c == 1 and back:
                        context_chunk(r, CHUNKS - 1)
                    if c == 2 and front:
                        transpose_c(f, attend)
                    if attend and c >= 2:
                        context_chunk(t, c - 2)
                    dense(t, c, front, attend, back, tail)

            iterations(pe, iteration)


def kernel(x, itok_B_3_7, itok_B_0_2, L0_cond_weight, L0_attn_Wq, L0_attn_Wk, L0_attn_Wv, L0_attn_Wo, L0_attn_cos,
           L0_attn_sin, L0_cond2_W, L0_cond2_lora_A, L0_cond2_lora_B_w, L0_ffn_W_base, L0_ffn_b_base,
           L0_ffn_W_router, L0_ffn_A, L0_ffn_B):
    import numpy as np
    import concourse.bacc as bacc
    from concourse.bass_utils import run_bass_kernel_spmd

    lay = np.ascontiguousarray
    a = {k: np.asarray(v) for k, v in locals().items() if k[0] in "xiL"}
    D = a["x"].shape[2]
    HD = a["L0_attn_cos"].shape[1]
    KV = a["L0_attn_Wk"].shape[1]
    GROUPS, PER = KV // HD, D // KV
    experts, _, rank = a["L0_ffn_B"].shape

    arrays = {
        "x": lay(a["x"]),
        "x_t": lay(a["x"].transpose(0, 2, 1)),
        "cond_ids": lay(a["itok_B_3_7"]),
        "lora_ids": lay(a["itok_B_0_2"]),
        "cond_w_t": lay(a["L0_cond_weight"].transpose(0, 2, 1)),
        "w_q": lay(a["L0_attn_Wq"].reshape(D, GROUPS, PER, HD).transpose(0, 2, 1, 3).reshape(D, D)),
        "w_kv": lay(np.concatenate([a["L0_attn_Wk"], a["L0_attn_Wv"]], axis=1)),
        "w_o": lay(a["L0_attn_Wo"].reshape(GROUPS, PER, HD, D).transpose(1, 0, 2, 3).reshape(D, D)),
        "cos": lay(a["L0_attn_cos"]),
        "sin": lay(a["L0_attn_sin"]),
        "w2_t": lay(a["L0_cond2_W"].T),
        "lora_a": lay(a["L0_cond2_lora_A"]),
        "lora_b_t": lay(a["L0_cond2_lora_B_w"].T),
        "base_t": lay(a["L0_ffn_W_base"].T),
        "base_bias": lay(a["L0_ffn_b_base"]),
        "router_t": lay(a["L0_ffn_W_router"].T),
        "experts_a_t": lay(a["L0_ffn_A"].reshape(experts * rank, D).T),
        "experts_b": lay(a["L0_ffn_B"].transpose(0, 2, 1).reshape(experts * rank, D)),
    }
    nc = bacc.Bacc("TRN2", target_bir_lowering=False, num_devices=1)
    aps = {n: nc.dram_tensor(n, v.shape, mybir.dt.from_np(v.dtype), kind="ExternalInput").ap()
           for n, v in arrays.items()}
    out = nc.dram_tensor("out", a["x"].shape, F32, kind="ExternalOutput").ap()
    build_program(nc, **aps, out=out)
    r = run_bass_kernel_spmd(nc, [arrays], core_ids=[0])
    return r.results[0]["out"]
```

```python
from contextlib import ExitStack

import concourse.bass as bass
from concourse import mybir

ALU = mybir.AluOpType
ACT = mybir.ActivationFunctionType
AX_X = mybir.AxisListType.X
F32 = mybir.dt.float32
F32R = mybir.dt.float32r
U32 = mybir.dt.uint32
I32 = mybir.dt.int32

P = 128
MASKED = -3.0e38


def build_program(nc, x, x_t, cond_ids, lora_ids, cond_w_t, w_q, w_kv, w_o, cos, sin, w2_t, lora_a, lora_b_t,
                  base_t, base_bias, router_t, experts_a_t, experts_b, out):
    BATCH, T, D = x.shape
    assert T == P
    KT = D // P
    HD = cos.shape[1]
    KV = w_kv.shape[1] // 2
    GROUPS = KV // HD
    PER = D // KV
    HEADS = GROUPS * PER
    PAIRS = GROUPS // 2
    assert KV == P and 2 * HD == 32
    CHUNKS = 2 * PER
    EXPERTS = router_t.shape[1]
    RANK = experts_a_t.shape[1] // EXPERTS
    LR = lora_a.shape[2]
    GATES = EXPERTS + EXPERTS * RANK
    NCOND, NLORA = cond_w_t.shape[0], lora_a.shape[0]
    QK = D + KV
    QKV = D + 2 * KV
    FFN = GATES + D
    FFN_X = FFN // 2
    FFN_Z = FFN - FFN_X
    SCORE_SCALE = float(HD) ** -0.5
    LORA_SCALE = 16 / 32
    MOE_SCALE = 32 / 16

    with ExitStack() as ctx:
        def sb(name, shape, dt=F32):
            return ctx.enter_context(nc.sbuf_tensor(name, shape, dt))

        def sem(name):
            return ctx.enter_context(nc.semaphore(name))

        assert P // LR == 4
        LOW_X, LOW_B, LOW_A = 1, 2, 3

        class Pair:

            def __init__(self, name, shape):
                self.hi, self.lo = sb(name + "_hi", shape, F32R), sb(name + "_lo", shape, F32R)

        bank = [ctx.enter_context(nc.psum_tensor(f"bank{i}", [P, 512], F32)) for i in range(8)]
        scores_ps = bank[0:2]
        probs_t_ps = bank[2]
        ctx_ps = bank[3]
        x_ps = bank[4]
        y_ps = bank[5]
        z_ps = bank[6]
        w_ps = bank[7]

        qkv_w = Pair("qkv_w", [P, KT, QKV])
        o_w = Pair("o_w", [P, KT, D])
        w2 = Pair("w2", [P, KT, D])
        ffn_w = Pair("ffn_w", [P, KT, FFN])
        lora_b = sb("lora_b", [P, D], F32R)
        moe_b = Pair("moe_b", [P, D])
        stage_a = sb("stage_a", [P, KT * QKV])
        stage_b = sb("stage_b", [P, KT * D])
        spare = sb("spare", [P, 2, D])
        stage_c = spare
        cond_raw = sb("cond_raw", [P, KT, D])
        cond_w = Pair("cond_w", [P, KT, D])
        a_raw = sb("a_raw", [P, KT, LR])
        lora_aw = sb("lora_aw", [P, KT, P // LR, LR], F32R)
        bias_row = sb("bias_row", [P, D])
        ids = sb("ids", [1, 2 * BATCH], I32)

        ident = sb("ident", [P, P])
        causal = sb("causal", [P, P])
        own_pair = sb("own_pair", [P, PAIRS])
        rope_cos = sb("rope_cos", [P, HD])
        rope_sin = sb("rope_sin", [P, HD])
        expert_no = sb("expert_no", [P, EXPERTS])

        xt_raw = sb("xt_raw", [P, KT, P])
        xt = Pair("xt", [P, KT, P])
        x_nat = sb("x_nat", [P, D])
        turn = sb("turn", [P, D])
        c_t = Pair("c_t", [P, KT, P])
        rope_a = sb("rope_a", [P, QK])
        rope_b = sb("rope_b", [P, QK])
        qk = rope_b
        q_pairs = sb("q_pairs", [P, 2, PER * P])
        k_pairs = sb("k_pairs", [P, 2, 2, P])
        q_t = [sb(f"q_t{e}", [P, PER, P], F32R) for e in range(2)]
        k_t = sb("k_t", [P, 2, 2, P])
        k_diag = Pair("k_diag", [P, GROUPS, P])
        v_nat = sb("v_nat", [P, KV])
        v_pad = [sb(f"v_pad{e}", [P, PAIRS, 2, HD]) for e in range(2)]
        waited = sb("waited", [1, CHUNKS])
        neg_max = sb("neg_max", [P, HEADS])
        sums = sb("sums", [P, HEADS])
        inv_sum = sb("inv_sum", [P, HEADS])
        probs = [sb(f"probs{i}", [P, PAIRS, P]) for i in range(2)]
        probs_t = [sb(f"probs_t{i}", [P, PAIRS, P]) for i in range(2)]
        inv_wide, ctx_n = spare[:, 0, :], spare[:, 1, :]
        inv_t = rope_a[:, 0:D]
        ctx_t = Pair("ctx_t", [P, PER, P])
        x1 = sb("x1", [P, D])
        x1_bias = stage_b[:, 0:D]
        x1_t = Pair("x1_t", [P, KT, P])
        low_t = sb("low_t", [P, P], F32R)
        c2_t = Pair("c2_t", [P, KT, P])
        gates = sb("gates", [P, GATES])
        top = sb("top", [P, 8])
        top_at = sb("top_at", [P, 8], U32)
        top_no = sb("top_no", [P, 2])
        neg_top = sb("neg_top", [P, 1])
        top_less = sb("top_less", [P, 2])
        top_exp = sb("top_exp", [P, 2])
        top_sum = sb("top_sum", [P, 1])
        top_inv = sb("top_inv", [P, 1])
        top_w = sb("top_w", [P, 2])
        pick = sb("pick", [P, 2, EXPERTS])
        gate = sb("gate", [P, EXPERTS])
        hidden = stage_b[:, D:D + EXPERTS * RANK]
        hidden_t = Pair("hidden_t", [P, P])
        out_sb = sb("out_sb", [P, D])

        ids_in, tables_in, bias_in = sem("ids_in"), sem("tables_in"), sem("bias_in")
        cond_in, xt_in, x_in, a_in = sem("cond_in"), sem("xt_in"), sem("x_in"), sem("a_in")
        qkv_in = [sem(f"qkv_in{k}") for k in range(KT)]
        o_in, w2_in, ffn_in, b_in = sem("o_in"), sem("w2_in"), sem("ffn_in"), sem("b_in")
        out_free = sem("out_free")
        zeroed, tables_made, sin_signed = sem("zeroed"), sem("tables_made"), sem("sin_signed")
        qkv_hi, o_hi, w2_hi, ffn_hi, b_hi = sem("qkv_hi"), sem("o_hi"), sem("w2_hi"), sem("ffn_hi"), sem("b_hi")
        qkv_lo, o_lo, w2_lo, ffn_lo, b_lo = sem("qkv_lo"), sem("o_lo"), sem("w2_lo"), sem("ffn_lo"), sem("b_lo")
        cond_hi, cond_lo, xt_hi, xt_lo = sem("cond_hi"), sem("cond_lo"), sem("xt_hi"), sem("xt_lo")
        cond_lo_first, rope_mul_first, qk_first = (sem("cond_lo_first"), sem("rope_mul_first"),
                                                   sem("qk_first"))
        cond_first_in = [sem(f"cond_first_in{k}") for k in range(KT)]
        a_hi, a_lo = sem("a_hi"), sem("a_lo")
        c_done, c_copied, ct_done, ct_hi, ct_lo = (sem("c_done"), sem("c_copied"), sem("ct_done"), sem("ct_hi"),
                                                   sem("ct_lo"))
        q_done, kv_done = sem("q_done"), sem("kv_done")
        rope_mul, v_copied, v_ready, qk_ready = sem("rope_mul"), sem("v_copied"), sem("v_ready"), sem("qk_ready")
        q_hi, k_hi, qk_lo, kt_done, qt_done = (sem("q_hi"), sem("k_hi"), sem("qk_lo"), sem("kt_done"),
                                               sem("qt_done"))
        kt_copied, kd_first, kd_ready, qt_ready = (sem("kt_copied"), sem("kd_first"), sem("kd_ready"),
                                                   sem("qt_ready"))
        scored, maxed, exped, pt_done = sem("scored"), sem("maxed"), sem("exped"), sem("pt_done")
        pt_even, pt_odd, ctx_done = sem("pt_even"), sem("pt_odd"), sem("ctx_done")
        inverted, inv_ready, inv_t_done, inv_t_ready = (sem("inverted"), sem("inv_ready"), sem("inv_t_done"),
                                                        sem("inv_t_ready"))
        ctx_normed, ctx_hi, ctx_lo = sem("ctx_normed"), sem("ctx_hi"), sem("ctx_lo")
        attn_done, x1_ready, x1b_ready = sem("attn_done"), sem("x1_ready"), sem("x1b_ready")
        x1t_done, x1t_hi, x1t_lo = sem("x1t_done"), sem("x1t_hi"), sem("x1t_lo")
        low_done, low_hi, low_lo = sem("low_done"), sem("low_hi"), sem("low_lo")
        c2_done, c2_copied, c2t_done, c2t_hi, c2t_lo = (sem("c2_done"), sem("c2_copied"), sem("c2t_done"),
                                                        sem("c2t_hi"), sem("c2t_lo"))
        x_base_added = sem("x_base_added")
        gates_done, gating, top_exped, hidden_ready = (sem("gates_done"), sem("gating"), sem("top_exped"),
                                                       sem("hidden_ready"))
        ht_done, ht_hi, ht_lo, ffn_done, out_ready = (sem("ht_done"), sem("ht_hi"), sem("ht_lo"), sem("ffn_done"),
                                                      sem("out_ready"))

        f32 = lambda ap: ap.bitcast(F32)
        flat = lambda t: t[:, :, :].rearrange("p a b -> p (a b)")

        def iterations(eng, iteration):
            iteration(-2, prep=True)
            iteration(-1, prep=True, front=True)
            iteration(0, prep=True, front=True, attend=True)
            iteration(1, prep=True, front=True, attend=True, back=True)
            with eng.Fori(2, BATCH - 2) as t:
                iteration(t, prep=True, front=True, attend=True, back=True, tail=True)
            iteration(BATCH - 2, front=True, attend=True, back=True, tail=True)
            iteration(BATCH - 1, attend=True, back=True, tail=True)
            iteration(BATCH, back=True, tail=True)
            iteration(BATCH + 1, tail=True)

        def wait_rotated(eng, f):
            if isinstance(f, int) and f == 0:
                eng.wait_ge(qk_first, 2)
            else:
                eng.wait_ge(qk_ready, 2 * f)

        q_columns = qk[:, 0:D].rearrange("s (b e d) -> s e b d", e=2, d=HD)
        k_columns = qk[:, D:QK].rearrange("s (j e d) -> s e j d", e=2, d=HD)

        def q_half(half):
            return q_pairs[:, :, :].rearrange("s e (b h d) -> s h e b d", h=2, d=HD)[:, half]

        def k_half(half, twin):
            return k_pairs[:, :, half, :].rearrange("s e (j h d) -> s h e j d", h=2, d=HD)[:, twin]

        block = ctx.enter_context(nc.Block())

        @block.sync
        def _(sp):
            def iteration(t, prep=False, front=False, attend=False, back=False, tail=False):
                g, f, r = t + 2, t + 1, t - 1
                if prep:
                    n = sp.value_load(ids[0:1, bass.ds(g, 1)], min_val=0, max_val=NCOND - 1)
                if prep and front:
                    if attend:
                        sp.wait_ge(cond_lo, KT * (g - 1))
                    else:
                        sp.wait_ge(cond_lo_first, KT)
                    sp.wait_ge(xt_lo, g)
                    sp.wait_ge(ids_in, 32)
                    sp.dma_start(cond_raw[:, :, :],
                                 cond_w_t[bass.ds(n, 1), :, :].rearrange("a (k p) o -> p (a k) o", p=P)
                                 ).then_inc(cond_in, 16)
                    sp.dma_start(xt_raw[:, :, :], x_t[bass.ds(g, 1), :, :].rearrange("a (k p) s -> p (a k) s", p=P)
                                 ).then_inc(xt_in, 16)
                if prep and not front:
                    for k in range(KT):
                        sp.dma_start(cond_raw[:, k:k + 1, :], cond_w_t[bass.ds(n, 1), k * P:(k + 1) * P, :]
                                     .rearrange("a p o -> p a o")).then_inc(cond_first_in[k], 16)
                    for k in range(KT):
                        sp.dma_start(stage_qkv[:, k, 0:D], w_q[k * P:(k + 1) * P, :]).then_inc(qkv_in[k], 16)
                    sp.dma_start(rope_cos[:, :], cos[0:P, :]).then_inc(tables_in, 16)
                    sp.dma_start(rope_sin[:, :], sin[0:P, :]).then_inc(tables_in, 16)
                if front and not attend:
                    sp.wait_ge(qkv_lo, KT)
                    stage_ffn = stage_a[:, 0:KT * FFN].rearrange("p (k n) -> p k n", k=KT)
                    for src, at in ((router_t, 0), (experts_a_t, EXPERTS), (base_t, GATES)):
                        sp.dma_start(stage_ffn[:, :, at:at + src.shape[1]], src.rearrange("(k p) n -> p k n", p=P)
                                     ).then_inc(ffn_in, 16)
                    stage_3 = stage_b[:, :].rearrange("p (k n) -> p k n", k=KT)
                    sp.dma_start(stage_3, w_o.rearrange("(k p) n -> p k n", p=P)).then_inc(o_in, 16)
                    sp.dma_start(bias_row[:, :], base_bias.partition_broadcast(P)).then_inc(bias_in, 16)
                    for n in range(P // LR):
                        sp.dma_start(stage_c[n * LR:(n + 1) * LR, 0, :], lora_b_t).then_inc(b_in, 16)
                    sp.dma_start(stage_c[:, 1, :], experts_b).then_inc(b_in, 16)
                if attend and not back:
                    sp.wait_ge(o_lo, 1)
                    stage_3 = stage_b[:, :].rearrange("p (k n) -> p k n", k=KT)
                    sp.dma_start(stage_3, w2_t.rearrange("(k p) n -> p k n", p=P)).then_inc(w2_in, 16)
                if attend:
                    n = sp.value_load(ids[0:1, bass.ds(t + BATCH, 1)], min_val=0, max_val=NLORA - 1)
                    if back:
                        sp.wait_ge(x1_ready, t)
                        sp.wait_ge(a_lo, t)
                        sp.wait_ge(ids_in, 32)
                    sp.dma_start(x_nat[:, :], x[bass.ds(t, 1), :, :].rearrange("a s d -> s (a d)")).then_inc(x_in, 16)
                    sp.dma_start(a_raw[:, :, :], lora_a[bass.ds(n, 1), :, :].rearrange("a (k p) r -> p (a k) r", p=P)
                                 ).then_inc(a_in, 16)
                if tail:
                    sp.wait_ge(out_ready, t - 1)
                    sp.wait_ge(ids_in, 32)
                    sp.dma_start(out[bass.ds(t - 2, 1), :, :].rearrange("a s d -> s (a d)"), out_sb[:, :]
                                 ).then_inc(out_free, 16)

            sp.dma_start(ids[0:1, 0:BATCH], cond_ids.rearrange("(a n) -> a n", a=1)).then_inc(ids_in, 16)
            sp.dma_start(ids[0:1, BATCH:2 * BATCH], lora_ids.rearrange("(a n) -> a n", a=1)).then_inc(ids_in, 16)
            sp.dma_start(xt_raw[:, :, :], x_t[0:1, :, :].rearrange("a (k p) s -> p (a k) s", p=P)).then_inc(xt_in, 16)
            stage_qkv = stage_a[:, :].rearrange("p (k n) -> p k n", k=KT)
            for k in range(KT):
                sp.dma_start(stage_qkv[:, k, D:QKV], w_kv[k * P:(k + 1) * P, :]).then_inc(qkv_in[k], 16)
            sp.wait_ge(ids_in, 32)
            iterations(sp, iteration)
            sp.wait_ge(out_free, 16 * (BATCH + 1))

        @block.gpsimd
        def _(pool):
            def tables():
                pool.memset(ident[:, :], 0.0).then_inc(zeroed, 1)
                pool.memset(causal[:, :], 0.0).then_inc(zeroed, 1)
                pool.memset(own_pair[:, :], 1.0).then_inc(zeroed, 1)
                pool.wait_ge(zeroed, 3)
                pool.affine_select(out=ident[:, :], in_=ident[:, :], compare_op=ALU.not_equal, fill=1.0, base=0,
                                   pattern=[[-1, P]], channel_multiplier=1).then_inc(tables_made, 1)
                pool.affine_select(out=causal[:, :], in_=causal[:, :], compare_op=ALU.is_ge, fill=MASKED,
                                   base=0, pattern=[[-1, P]], channel_multiplier=1).then_inc(tables_made, 1)
                pool.affine_select(out=own_pair[:, :], in_=own_pair[:, :], compare_op=ALU.is_ge, fill=0.0, base=0,
                                   pattern=[[-2 * HD, PAIRS]], channel_multiplier=1).then_inc(tables_made, 1)
                pool.wait_ge(tables_made, 3)
                pool.affine_select(out=own_pair[:, :], in_=own_pair[:, :], compare_op=ALU.is_ge, fill=0.0,
                                   base=2 * HD - 1, pattern=[[2 * HD, PAIRS]], channel_multiplier=-1
                                   ).then_inc(tables_made, 1)

            def clear():
                for e in range(2):
                    pool.memset(v_pad[e][:, :, :, :], 0.0).then_inc(zeroed, 1)
                pool.iota(expert_no[:, :], [[1, EXPERTS]], base=0, channel_multiplier=0,
                          allow_small_or_imprecise_dtypes=True).then_inc(zeroed, 1)
                pool.memset(out_sb[:, :], 0.0).then_inc(out_free, 16)

            def spread_k(f, e, half, again):
                if not again and e == 0:
                    return
                if half == 0:
                    pool.wait_ge(kt_copied, f + 1)
                if half == 0 and again:
                    pool.wait_ge(scored, CHUNKS * f - 1 + e)
                diag = k_diag.lo if half else k_diag.hi
                pool.tensor_tensor(diag[:, e * PAIRS:(e + 1) * PAIRS, :],
                                   k_t[:, e, half, :].unsqueeze(1).broadcast_to([P, PAIRS, P]),
                                   own_pair[:, :].unsqueeze(2).broadcast_to([P, PAIRS, P]), ALU.mult
                                   ).then_inc(kd_ready, 1)

            def iteration(t, prep=False, front=False, attend=False, back=False, tail=False):
                g, f, r = t + 2, t + 1, t - 1

                def split_cond(k):
                    pool.wait_ge(cond_hi, KT * g + k + 1)
                    pool.tensor_tensor(cond_w.lo[:, k, :], cond_raw[:, k, :], f32(cond_w.hi[:, k, :]), ALU.subtract
                                       ).then_inc(cond_lo, 1)

                if attend and not back:
                    pool.wait_ge(o_hi, 1)
                    pool.tensor_tensor(flat(o_w.lo), stage_b[:, :], f32(flat(o_w.hi)), ALU.subtract).then_inc(o_lo, 1)
                if back:
                    pool.wait_ge(a_hi, r + 1)
                    pool.tensor_tensor(lora_aw[:, :, LOW_A, :], a_raw[:, :, :], f32(lora_aw[:, :, 0, :]),
                                       ALU.subtract).then_inc(a_lo, 1)
                if back and not tail:
                    pool.wait_ge(w2_hi, 1)
                    pool.tensor_tensor(flat(w2.lo), stage_b[:, :], f32(flat(w2.hi)), ALU.subtract).then_inc(w2_lo, 1)
                if prep and not front:
                    clear()
                if prep:
                    pool.wait_ge(xt_hi, g + 1)
                    pool.tensor_tensor(xt.lo[:, :, :], xt_raw[:, :, :], f32(xt.hi[:, :, :]), ALU.subtract
                                       ).then_inc(xt_lo, 1)
                def add_rotated(n, at, w):
                    pool.wait_ge(rope_mul, 2 * f + n - 1)
                    pool.tensor_tensor(qk[:, at:at + w], rope_a[:, at:at + w], rope_b[:, at:at + w], ALU.add
                                       ).then_inc(qk_ready, 1)

                if prep and front:
                    split_cond(0)
                if front and attend:
                    add_rotated(0, 0, D)
                if front and attend:
                    add_rotated(1, D, KV)
                if prep and front:
                    split_cond(1)
                if back:
                    pool.wait_ge(bias_in, 16)
                    pool.wait_ge(w2_lo, 1)
                    pool.wait_ge(x1_ready, r + 1)
                    if tail:
                        pool.wait_ge(out_ready, t - 1)
                    pool.tensor_tensor(x1_bias[:, :], x1[:, :], bias_row[:, :], ALU.add).then_inc(x1b_ready, 1)
                if prep and attend:
                    split_cond(2)
                if front:
                    for e in range(2):
                        for half in range(2):
                            spread_k(f, e, half, attend)
                if prep and front and not attend:
                    split_cond(2)
                if prep and front:
                    split_cond(3)
            tables()
            iterations(pool, iteration)

        @block.scalar
        def _(act):
            def copy(out, in_, scale=1.0):
                return nc.scalar.activation(out, in_, ACT.Copy, scale=scale)

            def exp_chunk(t, c):
                p, e = c // 2, c % 2
                for j in range(PAIRS):
                    h = p * GROUPS + 2 * j + e
                    act.wait_ge(maxed, PAIRS * (CHUNKS * t + c) + j + 1)
                    last = nc.scalar.activation(probs[c % 2][:, j, :], probs[c % 2][:, j, :], ACT.Exp,
                                                bias=neg_max[:, h:h + 1], scale=-1.0, accum_out=sums[:, h:h + 1])
                last.then_inc(exped, 1)

            def copy_q(f, e, again):
                act.wait_ge(qt_done, 2 * f + e + 1)
                if again:
                    act.wait_ge(scored, CHUNKS * f - 1 + e)
                copy(flat(q_t[e]), y_ps[:, :], SCORE_SCALE).then_inc(qt_ready, 1)

            def exp_top(r):
                act.wait_ge(gating, 6 * r + 4)
                nc.scalar.activation(top_exp[:, :], top_less[:, :], ACT.Exp).then_inc(top_exped, 1)

            def evacuate_odd(b, c, again):
                act.wait_ge(pt_done, CHUNKS * b + c + 1)
                if c >= 2 or again:
                    act.wait_ge(ctx_done, CHUNKS * b + c - 1)
                copy(flat(probs_t[1]), probs_t_ps[:, :]).then_inc(pt_odd, 1)

            def iteration(t, prep=False, front=False, attend=False, back=False, tail=False):
                g, f, r = t + 2, t + 1, t - 1

                def split_cond(k):
                    if front:
                        act.wait_ge(cond_in, 16 * g)
                    else:
                        act.wait_ge(cond_first_in[k], 16)
                    copy(cond_w.hi[:, k, :], cond_raw[:, k, :]).then_inc(cond_hi, 1)

                for c in range(CHUNKS):
                    if c == 5 and back:
                        act.wait_ge(low_done, r + 1)
                        copy(low_t[:, :], x_ps[:, 0:P], LORA_SCALE).then_inc(low_hi, 1)
                    if c == 4 and back:
                        act.wait_ge(x1t_done, r + 1)
                        copy(flat(x1_t.hi), x_ps[:, :]).then_inc(x1t_hi, 1)
                    if c == 1 and back:
                        act.wait_ge(inv_t_done, r + 1)
                        copy(inv_t, (x_ps if attend else y_ps)[:, :]).then_inc(inv_t_ready, 1)
                    if c == 1 and back and not attend:
                        exp_top(r - 1)
                    if c == 1 and tail:
                        act.wait_ge(ht_done, t - 1)
                        copy(hidden_t.hi[:, :], w_ps[:, 0:P]).then_inc(ht_hi, 1)
                    if c == 0 and attend:
                        copy_q(t, 1, back)
                    if c == 0 and back:
                        evacuate_odd(r, CHUNKS - 1, True)
                    if c == (0 if attend else 2) and back:
                        act.wait_ge(a_in, 16 * (r + 1))
                        copy(lora_aw[:, :, 0:LOW_A, :], a_raw[:, :, :].unsqueeze(2).broadcast_to([P, KT, LOW_A, LR])
                             ).then_inc(a_hi, 1)
                    if attend:
                        if c == 0 and back:
                            act.wait_ge(inverted, t)
                        exp_chunk(t, c)
                    if c == 1 and front:
                        act.wait_ge(c_done, f + 1)
                        copy(turn[:, :], y_ps[:, :]).then_inc(c_copied, 1)
                    if c == 6 and back:
                        act.wait_ge(c2_done, r + 1)
                        copy(turn[:, :], (z_ps if attend else scores_ps[1])[:, :]).then_inc(c2_copied, 1)
                    if attend and c in (2, 4, 6):
                        evacuate_odd(t, c - 1, back)
                    if c == 2 and front:
                        act.wait_ge(ct_done, f + 1)
                        copy(flat(c_t.hi), y_ps[:, :]).then_inc(ct_hi, 1)
                    if c == 2 and prep:
                        act.wait_ge(xt_in, 16 * (g + 1))
                        copy(flat(xt.hi), flat(xt_raw)).then_inc(xt_hi, 1)
                    if c == 5 and front:
                        if not attend:
                            act.wait_ge(qk_first, 1)
                        else:
                            act.wait_ge(qk_ready, 2 * f - 1)
                        copy(q_half(0).bitcast(F32R), q_columns).then_inc(q_hi, 1)
                    if c in (2, 3, 4) and prep:
                        split_cond(c - 2)
                    if c == 7 and prep:
                        split_cond(3)
                    if c == 7 and prep and not front:
                        for k in range(KT):
                            act.wait_ge(qkv_in[k], 32)
                            copy(qkv_w.hi[:, k, :], stage_a[:, k * QKV:(k + 1) * QKV]).then_inc(qkv_hi, 1)
                    if c == 5 and front and not attend:
                        act.wait_ge(ffn_in, 48)
                        copy(flat(ffn_w.hi), stage_a[:, 0:KT * FFN]).then_inc(ffn_hi, 1)
                    if c == 0 and attend and not back:
                        act.wait_ge(o_in, 16)
                        copy(flat(o_w.hi), stage_b[:, :]).then_inc(o_hi, 1)
                    if c == 3 and attend and not back:
                        act.wait_ge(b_in, 16 * (P // LR + 1))
                        copy(lora_b[:, :], stage_c[:, 0, :]).then_inc(b_hi, 1)
                        copy(moe_b.hi[:, :], stage_c[:, 1, :]).then_inc(b_hi, 1)
                    if c == 2 and back and not tail:
                        act.wait_ge(w2_in, 16)
                        copy(flat(w2.hi), stage_b[:, :]).then_inc(w2_hi, 1)
                    if c == (7 if attend and not front else 6) and back:
                        act.wait_ge(c2t_done, r + 1)
                        copy(flat(c2_t.hi), x_ps[:, :]).then_inc(c2t_hi, 1)
                    if c == 6 and front:
                        act.wait_ge(kt_done, f + 1)
                        if attend:
                            act.wait_ge(kd_ready, 4 * f - 2)
                        copy(k_t[:, :, :, :].rearrange("q e h s -> q (e h s)"), w_ps[:, :]).then_inc(kt_copied, 1)
                        copy_q(f, 0, attend)
                    if c == 7 and back and (front or not attend):
                        exp_top(r)

            iterations(act, iteration)

        @block.vector
        def _(dve):
            def low_of(pair_lo, value, pair_hi):
                return nc.vector.tensor_tensor(pair_lo, value, f32(pair_hi), ALU.subtract)

            def max_chunk(t, c, again):
                dve.wait_ge(scored, CHUNKS * t + c + 1)
                if c >= 2 or again:
                    dve.wait_ge(pt_done, CHUNKS * t + c - 1)
                nc.vector.memset(waited[0:1, c:c + 1], 0.0)
                p, e = c // 2, c % 2
                for j in range(PAIRS):
                    h = p * GROUPS + 2 * j + e
                    nc.vector.tensor_tensor_reduce(probs[c % 2][:, j, :], scores_ps[c % 2][:, j * P:(j + 1) * P],
                                                   causal[:, :], -1.0, -MASKED, ALU.add, ALU.min,
                                                   neg_max[:, h:h + 1]).then_inc(maxed, 1)

            def evacuate_even(t, c, again):
                dve.wait_ge(pt_done, CHUNKS * t + c + 1)
                if c >= 2 or again:
                    dve.wait_ge(ctx_done, CHUNKS * t + c - 1)
                nc.vector.tensor_copy(flat(probs_t[0]), probs_t_ps[:, :]).then_inc(pt_even, 1)

            def rotate(src, at, n):
                half = HD // 2
                head = lambda tile, at: tile[:, at:at + n * HD].rearrange("s (h d) -> s h d", d=HD)
                tab = lambda tile, lo, w: tile[:, lo:lo + w].unsqueeze(1).broadcast_to([P, n, w])
                nc.vector.tensor_tensor(head(rope_a, at), head(src, 0), tab(rope_cos, 0, HD), ALU.mult)
                for to, frm in ((0, half), (half, 0)):
                    last = nc.vector.tensor_tensor(head(rope_b, at)[:, :, to:to + half],
                                                   head(src, 0)[:, :, frm:frm + half],
                                                   tab(rope_sin, to, half), ALU.mult)
                return last

            def add_rotated(at, w, n):
                dve.wait_ge(rope_mul_first, n)
                nc.vector.tensor_tensor(qk[:, at:at + w], rope_a[:, at:at + w], rope_b[:, at:at + w], ALU.add
                                        ).then_inc(qk_first, 1)

            def invert(r):
                dve.wait_ge(exped, CHUNKS * (r + 1))
                nc.vector.reciprocal(inv_sum[:, :], sums[:, :]).then_inc(inverted, 1)
                dve.wait_ge(b_lo, 2)
                dve.wait_ge(inverted, r + 1)
                nc.vector.tensor_copy(inv_wide.rearrange("s (h d) -> s h d", d=HD),
                                      inv_sum[:, :].unsqueeze(2).broadcast_to([P, HEADS, HD])).then_inc(inv_ready, 1)

            def split_k(f):
                wait_rotated(dve, f)
                if not (isinstance(f, int) and f == 0):
                    dve.wait_ge(kt_done, f)
                for twin in range(2):
                    last = nc.vector.tensor_copy(k_half(0, twin).bitcast(F32R), k_columns)
                last.then_inc(k_hi, 1)
                dve.wait_ge(k_hi, f + 1)
                for twin in range(2):
                    nc.vector.tensor_tensor(k_half(1, twin), k_columns, k_half(0, twin), ALU.subtract)

            def split_q(f):
                dve.wait_ge(q_hi, f + 1)
                nc.vector.tensor_tensor(q_half(1), q_columns, q_half(0), ALU.subtract).then_inc(qk_lo, 1)

            def spread_k_first(half):
                diag = k_diag.lo if half else k_diag.hi
                nc.vector.tensor_tensor(diag[:, 0:PAIRS, :],
                                        k_t[:, 0, half, :].unsqueeze(1).broadcast_to([P, PAIRS, P]),
                                        own_pair[:, :].unsqueeze(2).broadcast_to([P, PAIRS, P]), ALU.mult
                                        ).then_inc(kd_first, 1)

            def normalise(r):
                dve.wait_ge(inv_t_ready, r + 1)
                dve.wait_ge(ctx_done, CHUNKS * (r + 1))
                nc.vector.tensor_tensor(ctx_n, ctx_ps[:, :], inv_t, ALU.mult).then_inc(ctx_normed, 1)

            def split_high(r):
                dve.wait_ge(ctx_normed, r + 1)
                nc.vector.tensor_copy(flat(ctx_t.hi), ctx_n).then_inc(ctx_hi, 1)

            def split_low(r):
                dve.wait_ge(ctx_hi, r + 1)
                low_of(flat(ctx_t.lo), ctx_n, flat(ctx_t.hi)).then_inc(ctx_lo, 1)

            def pad_v(t, again):
                if again:
                    dve.wait_ge(ctx_done, CHUNKS * t)
                else:
                    dve.wait_ge(zeroed, 6)
                dve.wait_ge(v_copied, t + 1)
                v = v_nat[:, :].rearrange("s (j e d) -> s j e d", e=2, d=HD)
                for e in range(2):
                    nc.vector.tensor_copy(v_pad[e][:, :, e, :], v[:, :, e, :]).then_inc(v_ready, 1)

            def choose_experts(r):
                n = 6 * r
                dve.wait_ge(gates_done, r + 1)
                nc.vector.tensor_copy(gates[:, :], x_ps[:, 0:GATES]).then_inc(gating, 1)
                dve.wait_ge(gating, n + 1)
                nc.vector.tensor_reduce(neg_top[:, :], gates[:, 0:EXPERTS], AX_X, ALU.max, negate=True
                                        ).then_inc(gating, 1)
                nc.vector.max(top[:, :], gates[:, 0:EXPERTS]).then_inc(gating, 1)
                dve.wait_ge(gating, n + 3)
                nc.vector.tensor_scalar(top_less[:, :], top[:, 0:2], neg_top[:, 0:1], None, ALU.add
                                        ).then_inc(gating, 1)
                nc.vector.max_index(top_at[:, :], top[:, :], gates[:, 0:EXPERTS]).then_inc(gating, 1)
                dve.wait_ge(gating, n + 5)
                nc.vector.tensor_copy(top_no[:, :], top_at[:, 0:2]).then_inc(gating, 1)

            def add_x_base(r):
                dve.wait_ge(x1b_ready, r + 1)
                nc.vector.tensor_tensor(x1_bias[:, 0:D - FFN_Z], x_ps[:, GATES:FFN_X], x1_bias[:, 0:D - FFN_Z],
                                        ALU.add).then_inc(x_base_added, 1)

            def gate_hidden(r):
                n = 6 * r
                dve.wait_ge(top_exped, r + 1)
                nc.vector.tensor_reduce(top_sum[:, :], top_exp[:, :], AX_X, ALU.add).then_inc(hidden_ready, 1)
                dve.wait_ge(hidden_ready, n + 1)
                nc.vector.reciprocal(top_inv[:, :], top_sum[:, :]).then_inc(hidden_ready, 1)
                dve.wait_ge(hidden_ready, n + 2)
                nc.vector.tensor_scalar(top_w[:, :], top_exp[:, :], top_inv[:, 0:1], MOE_SCALE, ALU.mult, ALU.mult
                                        ).then_inc(hidden_ready, 1)
                dve.wait_ge(hidden_ready, n + 3)
                dve.wait_ge(gating, n + 6)
                for i in range(2):
                    last = nc.vector.tensor_scalar(pick[:, i, :], expert_no[:, :], top_no[:, i:i + 1],
                                                   top_w[:, i:i + 1], ALU.is_equal, ALU.mult)
                last.then_inc(hidden_ready, 1)
                dve.wait_ge(hidden_ready, n + 4)
                nc.vector.tensor_tensor(gate[:, :], pick[:, 0, :], pick[:, 1, :], ALU.add).then_inc(hidden_ready, 1)
                dve.wait_ge(hidden_ready, n + 5)
                nc.vector.tensor_tensor(hidden[:, :].rearrange("s (e n) -> s e n", n=RANK),
                                        gates[:, EXPERTS:GATES].rearrange("s (e n) -> s e n", n=RANK),
                                        gate[:, :].unsqueeze(2).broadcast_to([P, EXPERTS, RANK]), ALU.mult
                                        ).then_inc(hidden_ready, 1)

            def split_hidden(q):
                dve.wait_ge(ht_hi, q + 1)
                low_of(hidden_t.lo[:, :], w_ps[:, 0:P], hidden_t.hi[:, :]).then_inc(ht_lo, 1)

            def add_out(q):
                dve.wait_ge(ffn_done, q + 1)
                dve.wait_ge(x_base_added, q + 1)
                dve.wait_ge(out_free, 16 * (q + 1))
                in_x = D - FFN_Z
                nc.vector.tensor_tensor(out_sb[:, in_x:], z_ps[:, 0:FFN_Z], x1_bias[:, in_x:], ALU.add)
                nc.vector.tensor_tensor(out_sb[:, 0:in_x], z_ps[:, FFN_Z:D], x1_bias[:, 0:in_x], ALU.add
                                        ).then_inc(out_ready, 1)

            def iteration(t, prep=False, front=False, attend=False, back=False, tail=False):
                f, r = t + 1, t - 1
                drain = back and not attend
                if prep and not front:
                    for k in range(KT):
                        dve.wait_ge(cond_hi, k + 1)
                        low_of(cond_w.lo[:, k, :], cond_raw[:, k, :], cond_w.hi[:, k, :]).then_inc(cond_lo_first, 1)
                    for k in range(KT):
                        dve.wait_ge(qkv_hi, k + 1)
                        low_of(qkv_w.lo[:, k, :], stage_a[:, k * QKV:(k + 1) * QKV], qkv_w.hi[:, k, :]
                               ).then_inc(qkv_lo, 1)
                    dve.wait_ge(tables_in, 32)
                    nc.vector.tensor_scalar(rope_sin[:, 0:HD // 2], rope_sin[:, 0:HD // 2], -1.0, None, ALU.mult
                                            ).then_inc(sin_signed, 1)
                if attend and not back:
                    dve.wait_ge(zeroed, 6)
                    dve.wait_ge(tables_made, 4)
                for c in range(CHUNKS):
                    if c == 2 and back:
                        split_high(r)
                    if c == 2 and attend:
                        evacuate_even(t, 0, back)
                    if c == 2 and back:
                        split_low(r)
                    if c == 2 and tail and not drain:
                        add_out(t - 2)
                    if c == 3 and front:
                        dve.wait_ge(ct_hi, f + 1)
                        low_of(flat(c_t.lo), y_ps[:, :], flat(c_t.hi)).then_inc(ct_lo, 1)
                    if c == 7 and back and not (attend and not front):
                        dve.wait_ge(c2t_hi, r + 1)
                        low_of(flat(c2_t.lo), x_ps[:, :], flat(c2_t.hi)).then_inc(c2t_lo, 1)
                    if c == 0 and back and attend:
                        invert(r)
                    if c == 5 and front:
                        dve.wait_ge(kv_done, f + 1)
                        if attend:
                            rotate(w_ps, D, GROUPS).then_inc(rope_mul, 1)
                        else:
                            rotate(w_ps, D, GROUPS).then_inc(rope_mul_first, 1)
                            add_rotated(D, KV, 2)
                        nc.vector.tensor_copy(v_nat[:, :], w_ps[:, KV:2 * KV]).then_inc(v_copied, 1)
                    if c == 6 and front:
                        split_k(f)
                    if attend:
                        max_chunk(t, c, back)
                    if c == 5 and back:
                        dve.wait_ge(low_hi, r + 1)
                        rows = slice(LOW_X * LR, (LOW_X + 1) * LR)
                        nc.vector.scalar_tensor_tensor(low_t[rows, :], x_ps[rows, 0:P], LORA_SCALE,
                                                       f32(low_t[rows, :]), ALU.mult, ALU.subtract
                                                       ).then_inc(low_lo, 1)
                    if c == 4 and back:
                        dve.wait_ge(x1t_hi, r + 1)
                        low_of(flat(x1_t.lo), x_ps[:, :], flat(x1_t.hi)).then_inc(x1t_lo, 1)
                    if c == 4 and drain:
                        add_out(t - 2)
                    if c == 2 and drain:
                        choose_experts(t - 2)
                        add_x_base(t - 2)
                    if c == (2 if drain else 0) and tail:
                        gate_hidden(t - 2)
                    if c == 1 and tail and not drain:
                        split_hidden(t - 2)
                    if c == 1 and back:
                        normalise(r)
                    if c == 1 and attend:
                        pad_v(t, back)
                    if c == 3 and back:
                        dve.wait_ge(attn_done, r + 1)
                        dve.wait_ge(x_in, 16 * (r + 1))
                        nc.vector.tensor_tensor(x1[:, :], (z_ps if attend else scores_ps[0])[:, :], x_nat[:, :], ALU.add
                                                ).then_inc(x1_ready, 1)
                    if c == 3 and drain:
                        split_hidden(t - 2)
                    if attend and c >= 3 and c % 2 == 1:
                        evacuate_even(t, c - 1, back)
                    if c == 7 and attend and not front:
                        invert(t)
                    if c == 7 and back and attend and not front:
                        dve.wait_ge(c2t_hi, r + 1)
                        low_of(flat(c2_t.lo), x_ps[:, :], flat(c2_t.hi)).then_inc(c2t_lo, 1)
                    if c == 4 and front:
                        dve.wait_ge(q_done, f + 1)
                        if attend:
                            dve.wait_ge(qk_lo, f)
                        else:
                            dve.wait_ge(sin_signed, 1)
                        if attend:
                            rotate(y_ps, 0, HEADS).then_inc(rope_mul, 1)
                        else:
                            rotate(y_ps, 0, HEADS).then_inc(rope_mul_first, 1)
                            add_rotated(0, D, 1)
                    if c == 6 and front:
                        split_q(f)
                    if c == 7 and front and not attend:
                        dve.wait_ge(tables_made, 4)
                        dve.wait_ge(kt_copied, 1)
                        for half in range(2):
                            spread_k_first(half)
                    if c == 7 and back and (front or not attend):
                        choose_experts(r)
                        add_x_base(r)
                    if attend and not back:
                        if c == 6:
                            dve.wait_ge(b_hi, 2)
                            rows = slice(LOW_B * LR, (LOW_B + 1) * LR)
                            low_of(lora_b[rows, :], stage_c[rows, 0, :], lora_b[rows, :]).then_inc(b_lo, 1)
                            low_of(moe_b.lo[:, :], stage_c[:, 1, :], moe_b.hi[:, :]).then_inc(b_lo, 1)
                    if back and not tail and c in (3, 4, 5, 6):
                        k = c - 3
                        raw = stage_a[:, 0:KT * FFN].rearrange("p (k n) -> p k n", k=KT)
                        dve.wait_ge(ffn_hi, 1)
                        low_of(ffn_w.lo[:, k, :], raw[:, k, :], ffn_w.hi[:, k, :]).then_inc(ffn_lo, 1)

            iterations(dve, iteration)

        @block.tensor
        def _(pe):
            def with_high(out, lhs, rhs, cols, ks=range(KT)):
                for k in ks:
                    nc.tensor.matmul(out, lhs.hi[:, k, :], rhs.hi[:, k, cols], start=(k == 0), stop=False)
                    mm = nc.tensor.matmul(out, lhs.hi[:, k, :], rhs.lo[:, k, cols], start=False, stop=False)
                return mm

            def with_low(out, lhs, rhs, cols, ks=range(KT), last=True):
                for k in ks:
                    mm = nc.tensor.matmul(out, lhs.lo[:, k, :], rhs.hi[:, k, cols], start=False,
                                          stop=(last and k == KT - 1))
                return mm

            def transposes(out, tile):
                for k in range(KT):
                    mm = nc.tensor.transpose(out[:, k * P:(k + 1) * P], tile[:, k * P:(k + 1) * P], ident[:, :])
                return mm

            def score_chunk(t, c, again):
                p, e = c // 2, c % 2
                if c < 2:
                    if c == 0 and not again:
                        pe.wait_ge(kd_first, 2)
                    else:
                        pe.wait_ge(kd_ready, 4 * t + 2 * c)
                    pe.wait_ge(qt_ready, 2 * t + c + 1)
                if c >= 2 or again:
                    pe.wait_ge(maxed, PAIRS * (CHUNKS * t + c - 1))
                for n, diag in enumerate((k_diag.hi, k_diag.lo)):
                    mm = nc.tensor.matmul(scores_ps[c % 2][:, :], q_t[e][:, p, :],
                                          diag[:, e * PAIRS:(e + 1) * PAIRS, :],
                                          start=(n == 0), stop=(n == 1))
                mm.then_inc(scored, 1)

            def transpose_probs(b, c, again):
                pe.wait_ge(exped, CHUNKS * b + c + 1)
                if c >= 1:
                    pe.wait_ge(pt_even if c % 2 else pt_odd, PER * b + (c + 1) // 2)
                elif again:
                    pe.wait_ge(pt_odd, PER * b)
                for j in range(PAIRS):
                    mm = nc.tensor.transpose(probs_t_ps[:, j * P:(j + 1) * P], probs[c % 2][:, j, :], ident[:, :])
                mm.then_inc(pt_done, 1)

            def context_chunk(b, c):
                p, e = c // 2, c % 2
                if c == 0:
                    pe.wait_ge(v_ready, 2 * (b + 1))
                pe.wait_ge(pt_odd if c % 2 else pt_even, PER * b + c // 2 + 1)
                for j in range(PAIRS):
                    mm = nc.tensor.matmul(ctx_ps[2 * HD * j:2 * HD * (j + 1), p * P:(p + 1) * P],
                                          v_pad[e][:, j, :, :], probs_t[c % 2][:, j, :], start=(e == 0),
                                          stop=(e == 1))
                mm.then_inc(ctx_done, 1)

            first_half, second_half = range(KT // 2), range(KT // 2, KT)

            def condition(f, attend, ks):
                if 0 in ks:
                    pe.wait_ge(xt_hi, f + 1)
                    pe.wait_ge(xt_lo, f + 1)
                    if attend:
                        pe.wait_ge(qt_ready, 2 * f)
                for k in ks:
                    pe.wait_ge(cond_hi, KT * f + k + 1)
                    if attend:
                        pe.wait_ge(cond_lo, KT * (f - 1) + k + 1)
                    else:
                        pe.wait_ge(cond_lo_first, k + 1)
                    with_high(y_ps[:, :], xt, cond_w, slice(0, D), ks=[k])
                    mm = with_low(y_ps[:, :], xt, cond_w, slice(0, D), ks=[k])
                if KT - 1 in ks:
                    mm.then_inc(c_done, 1)

            def transpose_c(f, attend):
                pe.wait_ge(c_copied, f + 1)
                if not attend:
                    pe.wait_ge(tables_made, 4)
                transposes(y_ps, turn).then_inc(ct_done, 1)

            def project_q(f, attend):
                pe.wait_ge(ct_hi, f + 1)
                pe.wait_ge(ct_lo, f + 1)
                for k in range(KT):
                    if not attend:
                        pe.wait_ge(qkv_lo, k + 1)
                    with_high(y_ps[:, :], c_t, qkv_w, slice(0, D), ks=[k])
                    mm = with_low(y_ps[:, :], c_t, qkv_w, slice(0, D), ks=[k])
                mm.then_inc(q_done, 1)

            def project_kv(f, attend):
                if attend:
                    pe.wait_ge(kt_copied, f)
                with_high(w_ps[:, 0:2 * KV], c_t, qkv_w, slice(D, QKV))
                with_low(w_ps[:, 0:2 * KV], c_t, qkv_w, slice(D, QKV)).then_inc(kv_done, 1)

            def transpose_k(f):
                pe.wait_ge(qk_lo, f + 1)
                pe.wait_ge(v_copied, f + 1)
                for e in range(2):
                    for half in range(2):
                        at = (2 * e + half) * P
                        mm = nc.tensor.transpose(w_ps[:, at:at + P], k_pairs[:, e, half, :], ident[:, :])
                mm.then_inc(kt_done, 1)

            def transpose_q(f, e):
                if e == 1:
                    pe.wait_ge(qt_ready, 2 * f + 1)
                for p in range(PER):
                    mm = nc.tensor.transpose(y_ps[:, p * P:(p + 1) * P], q_pairs[:, e, p * P:(p + 1) * P],
                                             ident[:, :])
                mm.then_inc(qt_done, 1)

            def transpose_inverse(r, attend):
                pe.wait_ge(inv_ready, r + 1)
                if attend and not (isinstance(r, int) and r == 0):
                    pe.wait_ge(x_base_added, r)
                transposes(x_ps if attend else y_ps, inv_wide).then_inc(inv_t_done, 1)

            def project_out(r, attend, tail):
                to = z_ps if attend else scores_ps[0]
                pe.wait_ge(o_lo, 1)
                if attend and tail:
                    pe.wait_ge(out_ready, r)
                if not attend:
                    pe.wait_ge(maxed, PAIRS * CHUNKS * BATCH)
                pe.wait_ge(ctx_hi, r + 1)
                with_high(to[:, :], ctx_t, o_w, slice(0, D))
                pe.wait_ge(ctx_lo, r + 1)
                with_low(to[:, :], ctx_t, o_w, slice(0, D)).then_inc(attn_done, 1)

            def transpose_x1(r, attend):
                if not attend:
                    pe.wait_ge(x_base_added, r)
                pe.wait_ge(x1_ready, r + 1)
                transposes(x_ps, x1).then_inc(x1t_done, 1)

            def project_low(r):
                pe.wait_ge(x1t_hi, r + 1)
                pe.wait_ge(x1t_lo, r + 1)
                pe.wait_ge(a_lo, r + 1)
                for k in range(KT):
                    for rows in (x1_t.hi, x1_t.lo):
                        mm = nc.tensor.matmul(x_ps[:, 0:P], lora_aw[:, k, :, :], rows[:, k, :],
                                              start=(k == 0 and rows is x1_t.hi),
                                              stop=(k == KT - 1 and rows is x1_t.lo))
                mm.then_inc(low_done, 1)

            def condition_2_high(to, r, ks):
                if 0 in ks:
                    pe.wait_ge(w2_lo, 1)
                    pe.wait_ge(x1t_hi, r + 1)
                with_high(to[:, :], x1_t, w2, slice(0, D), ks)

            def condition_2_low(to, ks):
                with_low(to[:, :], x1_t, w2, slice(0, D), ks, last=False)

            def add_lora(to, r):
                pe.wait_ge(b_lo, 2)
                pe.wait_ge(low_hi, r + 1)
                pe.wait_ge(low_lo, r + 1)
                nc.tensor.matmul(to[:, :], low_t[:, :], lora_b[:, :], start=False, stop=True).then_inc(c2_done, 1)

            def transpose_c2(r):
                pe.wait_ge(c2_copied, r + 1)
                transposes(x_ps, turn).then_inc(c2t_done, 1)

            def project_gates(r):
                pe.wait_ge(ffn_lo, KT)
                pe.wait_ge(c2t_hi, r + 1)
                pe.wait_ge(c2t_lo, r + 1)
                with_high(x_ps[:, 0:FFN_X], c2_t, ffn_w, slice(0, FFN_X))
                with_low(x_ps[:, 0:FFN_X], c2_t, ffn_w, slice(0, FFN_X)).then_inc(gates_done, 1)

            def ffn_base_high(r, ks=range(KT)):
                pe.wait_ge(ffn_lo, KT)
                pe.wait_ge(c2t_hi, r + 1)
                with_high(z_ps[:, 0:FFN_Z], c2_t, ffn_w, slice(FFN_X, FFN), ks)

            def ffn_base_low(ks=range(KT)):
                with_low(z_ps[:, 0:FFN_Z], c2_t, ffn_w, slice(FFN_X, FFN), ks, last=False)

            def transpose_hidden(q):
                pe.wait_ge(hidden_ready, 6 * (q + 1))
                nc.tensor.transpose(w_ps[:, 0:P], hidden[:, :], ident[:, :]).then_inc(ht_done, 1)

            def finish_ffn(q):
                pe.wait_ge(ht_hi, q + 1)
                for to, cols, first in ((z_ps[:, 0:FFN_Z], slice(D - FFN_Z, D), False),
                                        (z_ps[:, FFN_Z:D], slice(0, D - FFN_Z), True)):
                    nc.tensor.matmul(to, hidden_t.hi[:, :], moe_b.hi[:, cols], start=first, stop=False)
                    nc.tensor.matmul(to, hidden_t.hi[:, :], moe_b.lo[:, cols], start=False, stop=False)
                    if not first:
                        pe.wait_ge(ht_lo, q + 1)
                    mm = nc.tensor.matmul(to, hidden_t.lo[:, :], moe_b.hi[:, cols], start=False, stop=True)
                mm.then_inc(ffn_done, 1)

            def dense(t, c, front, attend, back, tail):
                f, r, q = t + 1, t - 1, t - 2
                drain = back and not attend
                c2_ps = scores_ps[1] if drain else z_ps
                if c == 1 and drain:
                    project_gates(q)
                if c == 0 and tail and not drain:
                    if back:
                        ffn_base_high(q, second_half)
                    ffn_base_low(second_half)
                if c == 0 and front:
                    condition(f, attend, first_half)
                if c == 0 and back:
                    transpose_inverse(r, attend)
                if c == 1 and tail and not drain:
                    finish_ffn(q)
                if c == 3 and front:
                    project_q(f, attend)
                if c == 3 and back:
                    if drain:
                        ffn_base_high(q)
                        transpose_hidden(q)
                        ffn_base_low()
                    transpose_x1(r, attend)
                    if drain:
                        finish_ffn(q)
                if c == 4 and front:
                    project_kv(f, attend)
                if c == 4 and back:
                    condition_2_high(c2_ps, r, range(1) if front else range(KT))
                    project_low(r)
                if c == 5 and back:
                    if front:
                        condition_2_high(c2_ps, r, range(1, KT // 2))
                    condition_2_low(c2_ps, first_half)
                if c == 6 and front:
                    transpose_k(f)
                    transpose_q(f, 0)
                if c == (7 if attend and not front else 6) and back:
                    transpose_c2(r)
                if c == 7 and back and (front or not attend):
                    if attend:
                        project_gates(r)
                        ffn_base_high(r, first_half)
                    else:
                        ffn_base_high(r, first_half)
                        project_gates(r)
                        ffn_base_high(r, second_half)
                    ffn_base_low(first_half)
                if c == 7 and front:
                    transpose_q(f, 1)

            def iteration(t, prep=False, front=False, attend=False, back=False, tail=False):
                f, r = t + 1, t - 1
                drain = back and not attend
                c2_ps = scores_ps[1] if drain else z_ps
                for c in range(CHUNKS):
                    if attend:
                        score_chunk(t, c, back)
                    if c == 0 and back:
                        transpose_probs(r, CHUNKS - 1, True)
                    if c == 1 and back:
                        context_chunk(r, CHUNKS - 2)
                        context_chunk(r, CHUNKS - 1)
                    if c == 1 and tail and not drain:
                        transpose_hidden(t - 2)
                    if c == 1 and front:
                        condition(f, attend, second_half)
                    if c == 3 and back:
                        project_out(r, attend, tail)
                    if c == 6 and back:
                        if front:
                            condition_2_high(c2_ps, r, second_half)
                        condition_2_low(c2_ps, second_half)
                        add_lora(c2_ps, r)
                    if attend and c >= 1:
                        transpose_probs(t, c - 1, back)
                    if c == 2 and front:
                        transpose_c(f, attend)
                    if attend and c % 2 == 1 and c >= 3:
                        context_chunk(t, c - 3)
                        context_chunk(t, c - 2)
                    dense(t, c, front, attend, back, tail)

            iterations(pe, iteration)


def kernel(x, itok_B_3_7, itok_B_0_2, L0_cond_weight, L0_attn_Wq, L0_attn_Wk, L0_attn_Wv, L0_attn_Wo, L0_attn_cos,
           L0_attn_sin, L0_cond2_W, L0_cond2_lora_A, L0_cond2_lora_B_w, L0_ffn_W_base, L0_ffn_b_base,
           L0_ffn_W_router, L0_ffn_A, L0_ffn_B):
    import numpy as np
    import concourse.bacc as bacc
    from concourse.bass_utils import run_bass_kernel_spmd

    lay = np.ascontiguousarray
    a = {k: np.asarray(v) for k, v in locals().items() if k[0] in "xiL"}
    D = a["x"].shape[2]
    HD = a["L0_attn_cos"].shape[1]
    KV = a["L0_attn_Wk"].shape[1]
    GROUPS, PER = KV // HD, D // KV
    experts, _, rank = a["L0_ffn_B"].shape

    arrays = {
        "x": lay(a["x"]),
        "x_t": lay(a["x"].transpose(0, 2, 1)),
        "cond_ids": lay(a["itok_B_3_7"]),
        "lora_ids": lay(a["itok_B_0_2"]),
        "cond_w_t": lay(a["L0_cond_weight"].transpose(0, 2, 1)),
        "w_q": lay(a["L0_attn_Wq"].reshape(D, GROUPS, PER, HD).transpose(0, 2, 1, 3).reshape(D, D)),
        "w_kv": lay(np.concatenate([a["L0_attn_Wk"], a["L0_attn_Wv"]], axis=1)),
        "w_o": lay(a["L0_attn_Wo"].reshape(GROUPS, PER, HD, D).transpose(1, 0, 2, 3).reshape(D, D)),
        "cos": lay(a["L0_attn_cos"]),
        "sin": lay(a["L0_attn_sin"]),
        "w2_t": lay(a["L0_cond2_W"].T),
        "lora_a": lay(a["L0_cond2_lora_A"]),
        "lora_b_t": lay(a["L0_cond2_lora_B_w"].T),
        "base_t": lay(a["L0_ffn_W_base"].T),
        "base_bias": lay(a["L0_ffn_b_base"]),
        "router_t": lay(a["L0_ffn_W_router"].T),
        "experts_a_t": lay(a["L0_ffn_A"].reshape(experts * rank, D).T),
        "experts_b": lay(a["L0_ffn_B"].transpose(0, 2, 1).reshape(experts * rank, D)),
    }
    nc = bacc.Bacc("TRN2", target_bir_lowering=False, num_devices=1)
    aps = {n: nc.dram_tensor(n, v.shape, mybir.dt.from_np(v.dtype), kind="ExternalInput").ap()
           for n, v in arrays.items()}
    out = nc.dram_tensor("out", a["x"].shape, F32, kind="ExternalOutput").ap()
    build_program(nc, **aps, out=out)
    r = run_bass_kernel_spmd(nc, [arrays], core_ids=[0])
    return r.results[0]["out"]
```
